# Optimizing a Trainium2 kernel written in Bass

```python
import numpy as np
import jax
import jax.numpy as jnp

def _softmax(x, axis=-1):
    return jax.nn.softmax(x, axis=axis)

def _gelu(x):
    return jax.nn.gelu(x, approximate=True)

def _silu(x):
    return jax.nn.silu(x)

def _sigmoid(x):
    return jax.nn.sigmoid(x)

def _layernorm(x, axis=-1, eps=1e-05):
    m = jnp.mean(x, axis=axis, keepdims=True)
    v = jnp.var(x, axis=axis, keepdims=True)
    return (x - m) / jnp.sqrt(v + eps)

def _scatter_add(tgt, idx, src, axis=0):
    return tgt.at[idx].add(src)

def _segment_sum(src, seg, n):
    return jax.ops.segment_sum(src, seg, n)
kernel_name = 'mk_seq_postln_d1_jaxref_r8_c85992'

def setup_inputs(seed: int=0):
    np.random.seed(seed)
    _w = jnp.asarray

    def _L0_attn_setup():
        import jax, jax.numpy as jnp
        import numpy as np
        DECAY = 0.95
        EPS = 1e-05
        B, T, D, L = (4, 512, 128, 2)

        def _layer_norm(x, w, b):
            mu = jnp.mean(x, axis=-1, keepdims=True)
            var = jnp.mean(jnp.square(x - mu), axis=-1, keepdims=True)
            return (x - mu) * jax.lax.rsqrt(var + EPS) * w + b

        def _time_mix_layer(x, ln_w, ln_b, Wk, Wv, Wr, Wo):
            normed = _layer_norm(x, ln_w, ln_b)
            k = jnp.einsum('btd,ed->bte', normed, Wk)
            v = jnp.einsum('btd,ed->bte', normed, Wv)
            r = jax.nn.sigmoid(jnp.einsum('btd,ed->bte', normed, Wr))
            kv = k * v

            def step(state, kv_t):
                state = DECAY * state + (1.0 - DECAY) * kv_t
                return (state, state)
            init = jnp.zeros((x.shape[0], x.shape[2]), dtype=x.dtype)
            _, states = jax.lax.scan(step, init, jnp.swapaxes(kv, 0, 1))
            y = r * jnp.swapaxes(states, 0, 1)
            y = jnp.einsum('btd,ed->bte', y, Wo)
            return x + y
        key = jax.random.key(seed)
        ks = jax.random.split(key, 7)
        scale = 1.0 / np.sqrt(D)
        return {'h': jax.random.normal(ks[0], (B, T, D), dtype=jnp.float32), 'ln_w': jnp.ones((L, D), dtype=jnp.float32), 'ln_b': jnp.zeros((L, D), dtype=jnp.float32), 'Wk': jax.random.normal(ks[1], (L, D, D), dtype=jnp.float32) * scale, 'Wv': jax.random.normal(ks[2], (L, D, D), dtype=jnp.float32) * scale, 'Wr': jax.random.normal(ks[3], (L, D, D), dtype=jnp.float32) * scale, 'Wo': jax.random.normal(ks[4], (L, D, D), dtype=jnp.float32) * scale}
    _L0_attn_in = _L0_attn_setup()

    def _L0_ffn_setup():
        import jax, jax.numpy as jnp
        import numpy as np
        B, T, C = (8, 256, 128)
        H = 512
        E = 8
        K = 2
        LOAD_FACTOR = 1.2
        N_LAYER = 12

        def _get_expert_inputs(x, logits, expert_capacity):
            Tt = logits.shape[0]
            Cc = x.shape[1]
            top_k_logits, expert_indices = jax.lax.top_k(logits, K)
            expert_probs = jax.nn.softmax(top_k_logits, axis=-1)
            ei = jnp.swapaxes(expert_indices, 0, 1).ravel()
            one_hot = jax.nn.one_hot(ei, E, dtype=jnp.int32)
            pos = jnp.cumsum(one_hot, axis=0) * one_hot - 1
            pos = pos.reshape(-1, Tt, E)
            pos = jnp.swapaxes(pos, 0, 1)
            pos = jnp.max(pos, axis=2)
            ei = jnp.swapaxes(ei.reshape(-1, Tt), 0, 1)
            buf = jnp.zeros((E, expert_capacity, Cc), x.dtype)
            xr = jnp.repeat(x, K, axis=0)
            expert_inputs = buf.at[ei.ravel(), pos.ravel()].add(xr)
            return (expert_probs, pos, ei, expert_inputs)
        key = jax.random.key(seed)
        ks = jax.random.split(key, 9)
        std = 0.02
        proj_std = 0.02 * (2 * N_LAYER) ** (-0.5)
        return {'x': jax.random.normal(ks[0], (B, T, C), jnp.float32), 'router_w': jax.random.normal(ks[1], (C, E), jnp.float32) * std, 'router_b': jnp.zeros((E,), jnp.float32), 'w_c_fc': jax.random.normal(ks[2], (E, C, H), jnp.float32) * std, 'b_c_fc': jnp.zeros((E, 1, H), jnp.float32), 'w_gate': jax.random.normal(ks[3], (E, C, H), jnp.float32) * std, 'b_gate': jnp.zeros((E, 1, H), jnp.float32), 'w_c_proj': jax.random.normal(ks[4], (E, H, C), jnp.float32) * proj_std, 'b_c_proj': jnp.zeros((E, 1, C), jnp.float32)}
    _L0_ffn_in = _L0_ffn_setup()
    _d = {'L0_attn_h': _L0_attn_in['h'], 'L0_attn_ln_w': _L0_attn_in['ln_w'], 'L0_attn_ln_b': _L0_attn_in['ln_b'], 'L0_attn_Wk': _L0_attn_in['Wk'], 'L0_attn_Wv': _L0_attn_in['Wv'], 'L0_attn_Wr': _L0_attn_in['Wr'], 'L0_attn_Wo': _L0_attn_in['Wo'], 'L0_ffn_router_w': _L0_ffn_in['router_w'], 'L0_ffn_router_b': _L0_ffn_in['router_b'], 'L0_ffn_w_c_fc': _L0_ffn_in['w_c_fc'], 'L0_ffn_b_c_fc': _L0_ffn_in['b_c_fc'], 'L0_ffn_w_gate': _L0_ffn_in['w_gate'], 'L0_ffn_b_gate': _L0_ffn_in['b_gate'], 'L0_ffn_w_c_proj': _L0_ffn_in['w_c_proj'], 'L0_ffn_b_c_proj': _L0_ffn_in['b_c_proj']}
    _x0 = _d['L0_attn_h']
    _d['L0_attn_h'] = jax.random.normal(jax.random.fold_in(jax.random.key(seed), 1), (4, 1024, 128), dtype=_x0.dtype)
    del _x0
    return _d

def reference(L0_attn_h, L0_attn_ln_w, L0_attn_ln_b, L0_attn_Wk, L0_attn_Wv, L0_attn_Wr, L0_attn_Wo, L0_ffn_router_w, L0_ffn_router_b, L0_ffn_w_c_fc, L0_ffn_b_c_fc, L0_ffn_w_gate, L0_ffn_b_gate, L0_ffn_w_c_proj, L0_ffn_b_c_proj):

    def _L0_attn_ref(h, ln_w, ln_b, Wk, Wv, Wr, Wo):
        import jax, jax.numpy as jnp
        import numpy as np
        DECAY = 0.95
        EPS = 1e-05
        B, T, D, L = (4, 512, 128, 2)

        def _layer_norm(x, w, b):
            mu = jnp.mean(x, axis=-1, keepdims=True)
            var = jnp.mean(jnp.square(x - mu), axis=-1, keepdims=True)
            return (x - mu) * jax.lax.rsqrt(var + EPS) * w + b

        def _time_mix_layer(x, ln_w, ln_b, Wk, Wv, Wr, Wo):
            normed = _layer_norm(x, ln_w, ln_b)
            k = jnp.einsum('btd,ed->bte', normed, Wk)
            v = jnp.einsum('btd,ed->bte', normed, Wv)
            r = jax.nn.sigmoid(jnp.einsum('btd,ed->bte', normed, Wr))
            kv = k * v

            def step(state, kv_t):
                state = DECAY * state + (1.0 - DECAY) * kv_t
                return (state, state)
            init = jnp.zeros((x.shape[0], x.shape[2]), dtype=x.dtype)
            _, states = jax.lax.scan(step, init, jnp.swapaxes(kv, 0, 1))
            y = r * jnp.swapaxes(states, 0, 1)
            y = jnp.einsum('btd,ed->bte', y, Wo)
            return x + y
        out = h
        for i in range(Wk.shape[0]):
            out = _time_mix_layer(out, ln_w[i], ln_b[i], Wk[i], Wv[i], Wr[i], Wo[i])
        return out

    def _L0_ffn_ref(x, router_w, router_b, w_c_fc, b_c_fc, w_gate, b_gate, w_c_proj, b_c_proj):
        import jax, jax.numpy as jnp
        import numpy as np
        B, T, C = (8, 256, 128)
        H = 512
        E = 8
        K = 2
        LOAD_FACTOR = 1.2
        N_LAYER = 12

        def _get_expert_inputs(x, logits, expert_capacity):
            Tt = logits.shape[0]
            Cc = x.shape[1]
            top_k_logits, expert_indices = jax.lax.top_k(logits, K)
            expert_probs = jax.nn.softmax(top_k_logits, axis=-1)
            ei = jnp.swapaxes(expert_indices, 0, 1).ravel()
            one_hot = jax.nn.one_hot(ei, E, dtype=jnp.int32)
            pos = jnp.cumsum(one_hot, axis=0) * one_hot - 1
            pos = pos.reshape(-1, Tt, E)
            pos = jnp.swapaxes(pos, 0, 1)
            pos = jnp.max(pos, axis=2)
            ei = jnp.swapaxes(ei.reshape(-1, Tt), 0, 1)
            buf = jnp.zeros((E, expert_capacity, Cc), x.dtype)
            xr = jnp.repeat(x, K, axis=0)
            expert_inputs = buf.at[ei.ravel(), pos.ravel()].add(xr)
            return (expert_probs, pos, ei, expert_inputs)
        Bb, Tt, Cc = x.shape
        logits = jnp.einsum('btc,ce->bte', x, router_w) + router_b
        cap = int(LOAD_FACTOR * K * Tt // E)
        probs, pos, idx, einp = jax.vmap(lambda xb, lb: _get_expert_inputs(xb, lb, cap))(x, logits)
        if Bb % E == 0:
            t = einp.reshape(E, Bb // E, E, cap, Cc)
            t = jnp.swapaxes(t, 0, 2)
        else:
            t = jnp.swapaxes(einp, 0, 1)
        einp2 = t.reshape(E, Bb * cap, Cc)
        h = jnp.einsum('eti,eih->eth', einp2, w_c_fc) + b_c_fc
        g = jnp.einsum('eti,eih->eth', einp2, w_gate) + b_gate
        o = jnp.einsum('eth,eho->eto', jax.nn.silu(h * g), w_c_proj) + b_c_proj
        if Bb % E == 0:
            o = o.reshape(E, Bb // E, E, cap, Cc)
            o = jnp.swapaxes(o, 0, 2)
            o = o.reshape(Bb, E, cap, Cc)
        else:
            o = o.reshape(E, Bb, cap, Cc)
            o = jnp.swapaxes(o, 0, 1)

        def collect(eo, i, p, pr):
            sel = eo[i, p]
            return jnp.sum(pr[..., None] * sel, axis=1)
        return jax.vmap(collect)(o, idx, pos, probs)
    x = L0_attn_h
    x = _layernorm(x + _L0_attn_ref(x, L0_attn_ln_w, L0_attn_ln_b, L0_attn_Wk, L0_attn_Wv, L0_attn_Wr, L0_attn_Wo), axis=-1)
    x = _layernorm(x + _L0_ffn_ref(x, L0_ffn_router_w, L0_ffn_router_b, L0_ffn_w_c_fc, L0_ffn_b_c_fc, L0_ffn_w_gate, L0_ffn_b_gate, L0_ffn_w_c_proj, L0_ffn_b_c_proj), axis=-1)
    return x

_drawn_inputs = setup_inputs


def setup_inputs(seed=0):
    import zlib

    import numpy as np

    out = dict(_drawn_inputs(seed))
    spreads = {'L0_attn_ln_w': (1.0, 0.2),
     'L0_attn_ln_b': (0.0, 0.55),
     'L0_ffn_router_b': (0.0, 0.1),
     'L0_ffn_b_c_fc': (0.0, 0.8),
     'L0_ffn_b_gate': (0.0, 0.8),
     'L0_ffn_b_c_proj': (0.0, 0.1)}
    factors = {'L0_ffn_w_c_fc': 8.0, 'L0_ffn_w_gate': 8.0, 'L0_ffn_w_c_proj': 8.0}
    for name, (base, spread) in spreads.items():
        noise = np.random.default_rng([zlib.crc32(name.encode()), seed]).standard_normal(out[name].shape)
        drawn = base * np.exp(spread * noise) if base else spread * noise
        out[name] = jnp.asarray(drawn.astype(out[name].dtype))
    for name, factor in factors.items():
        out[name] = (out[name] * factor).astype(out[name].dtype)
    return out
```

```python
from contextlib import ExitStack

import numpy as np
import concourse.bass as bass
from concourse import mybir

ALU = mybir.AluOpType
ACT = mybir.ActivationFunctionType
AX = mybir.AxisListType
F32 = mybir.dt.float32
BF16 = mybir.dt.bfloat16
U32 = mybir.dt.uint32

P = 128
B, T, L = 4, 1024, 2
TILES = T // P
HT = TILES // 2
HALF = HT * P
E, K, H = 8, 2, 512
HC = H // P
CAP = int(1.2 * K * T // E)
COLS = CAP + CAP % 2
PART = 104
PARTS = 3
SLOTS = PART * PARTS
GROUPS = -(-E * SLOTS // (4 * P))
ROWS = GROUPS * 4 * P
POINTS = E * HC
FAR = float(1 << 20)
EPS = 1e-5
DECAY = 0.95

assert CAP <= COLS <= SLOTS and L == 2 and K == 2

TENSOR_STAGES = {
    2: [("turn", 0)], 3: [("kvr", 0)], 4: [("turn", 1)], 5: [("kvr", 1)], 6: [("out", 0)], 7: [("out", 1)],
    9: [("turn", 2)], 10: [("kvr", 2)], 11: [("turn", 3)], 12: [("kvr", 3)], 13: [("out", 2)], 14: [("out", 3)],
    16: [("turn", 4)], 17: [("logits", 0)], 18: [("turn", 5)], 19: [("logits", 1)], 21: [("count", 0)],
}
SCALAR_STAGES = {
    2: [("turned", 0)], 3: [("kr", 0)], 4: [("turned", 1)], 5: [("kr", 1)],
    9: [("turned", 2)], 10: [("kr", 2)], 11: [("turned", 3)], 12: [("kr", 3)],
    16: [("turned", 4)], 18: [("turned", 5)], 21: [("lead", 0)],
}
VECTOR_STAGES = {
    0: [("stats", 0), ("stats", 1)], 1: [("norm", 0)], 2: [("norm", 1)], 4: [("mix", 0)], 6: [("mix", 1)],
    7: [("add", 0), ("stats", 2)], 8: [("add", 1), ("stats", 3), ("norm", 2)], 9: [("norm", 3)],
    11: [("mix", 2)], 13: [("mix", 3)],
    14: [("add", 2), ("stats", 4)], 15: [("add", 3), ("stats", 5), ("norm", 4)], 16: [("norm", 5)],
    18: [("top", 0)], 20: [("top", 1), ("choice", 0)], 22: [("rows", 0)],
}
VECTOR_COMBINE = {8: [("gather_sum", 0)], 9: [("final_norm", 0)], 12: [("gather_sum", 1)], 13: [("final_norm", 1)]}
POOL_STAGES = {
    0: [("rstd", 0), ("rstd", 1)], 7: [("rstd", 2)], 8: [("rstd", 3)], 9: [("skip_sum", 0)],
    14: [("keep", 0), ("rstd", 4)], 15: [("rstd", 5)], 22: [("shares", 0), ("scatter", 0)],
}
POOL_COMBINE = {1: [("gather", 0)], 2: [("gather", 1)], 9: [("final_rstd", 0)], 12: [("final_rstd", 1)]}


def nth(b, per, k):
    return b * per + k


def ahead(eng, *values):
    for value in values:
        if not isinstance(value, int):
            eng.compute_val(value)


def later(b):
    return not (isinstance(b, int) and b == 0)


def time_mix_moe(nc, h, ln_w, ln_b, Wk, Wv, Wr, Wo, router_w, router_b, w_fc, b_fc, w_gate, b_gate,
                 w_proj, b_proj, out):
    with ExitStack() as ctx:
        def sb(name, shape, dt=F32):
            return ctx.enter_context(nc.sbuf_tensor(name, shape, dt))

        def sem(name):
            return ctx.enter_context(nc.semaphore(name))

        ident = sb("ident", [P, P])
        upto = sb("upto", [P, P], BF16)
        ones = sb("ones", [P, P], BF16)
        decay = sb("decay", [P, HALF])
        power = sb("power", [P, HT])
        expert_id = sb("expert_id", [P, TILES * K * E])
        expert_base = sb("expert_base", [P, TILES * K * E])
        lnw_sb = sb("lnw_sb", [P, L])
        lnb_sb = sb("lnb_sb", [P, L])
        w_raw = sb("w_raw", [P, 4 * L, P])
        w_mix = sb("w_mix", [P, 4 * L, P])
        router_sb = sb("router_sb", [P, E])
        rbias_sb = sb("rbias_sb", [P, E])
        fc_sb = sb("fc_sb", [P, E, H])
        gate_sb = sb("gate_sb", [P, E, H])
        proj_sb = sb("proj_sb", [P, E, HC, P])
        bfc_sb = sb("bfc_sb", [P, E, HC])
        bgate_sb = sb("bgate_sb", [P, E, HC])
        bproj_sb = sb("bproj_sb", [P, E, P])
        x_in = sb("x_in", [P, TILES, P])
        x_mid = sb("x_mid", [P, TILES, P])
        x_skip = sb("x_skip", [P, TILES, P])
        x_sum = sb("x_sum", [P, TILES, P])
        normed = sb("normed", [P, TILES, P])
        stats = sb("stats", [P, 3, TILES, 6])
        moments = sb("moments", [P, 3, TILES, 2])
        shifted = sb("shifted", [P, 3, TILES])
        rstd = sb("rstd", [P, 3, TILES])
        normT = sb("normT", [P, T])
        k_sb = sb("k_sb", [P, T])
        gate_r = sb("gate_r", [P, T])
        kv_sb = sb("kv_sb", [P, T])
        state = sb("state", [P, T])
        mixed = sb("mixed", [P, T])
        x_ln = sb("x_ln", [P, TILES, P])
        x_old = sb("x_old", [P, TILES, P])
        logit = sb("logit", [P, TILES, E])
        top_v = sb("top_v", [P, TILES, 8])
        top_i = sb("top_i", [P, TILES, 8], U32)
        top_f = sb("top_f", [P, TILES, K])
        gap = sb("gap", [P, TILES])
        gap_t = sb("gap_t", [P, TILES])
        share = sb("share", [P, TILES, K])
        share_old = sb("share_old", [P, TILES, K])
        chosen = sb("chosen", [P, TILES, K, E], BF16)
        row_in = sb("row_in", [P, TILES * K * E])
        row_far = sb("row_far", [P, TILES * K * E])
        row_both = sb("row_both", [P, 2, TILES * K, E])
        row_f = sb("row_f", [P, 2, TILES * K])
        row_to = sb("row_to", [P, TILES * K], U32)
        row_from = sb("row_from", [P, TILES * K], U32)
        row_old = sb("row_old", [P, TILES * K], U32)
        slot_x = sb("slot_x", [P, GROUPS * 4, P])
        slotT = sb("slotT", [P, ROWS])
        gate_s = sb("gate_s", [P, 2, COLS])
        prod = sb("prod", [P, 2, HC, COLS])
        hidden = sb("hidden", [P, 2, HC, SLOTS])
        o_sb = sb("o_sb", [PART, E, PARTS, P])
        picked = sb("picked", [P, TILES, K, P])
        part_sum = sb("part_sum", [P, TILES, P])
        y_sum = sb("y_sum", [P, TILES, P])
        y_out = sb("y_out", [P, TILES, P])
        y_stats = sb("y_stats", [P, TILES, 6])
        y_moments = sb("y_moments", [P, TILES, 2])
        y_shifted = sb("y_shifted", [P, TILES])
        y_rstd = sb("y_rstd", [P, TILES])

        pair = [[ctx.enter_context(nc.psum_tensor(f"pair{i}{n}", [P, 512], F32)) for n in "gh"] for i in range(2)]
        ps_o = ctx.enter_context(nc.psum_tensor("ps_o", [P, 512], F32))
        bank = [ctx.enter_context(nc.psum_tensor(f"bank{i}", [P, 512], F32)) for i in range(3)]

        slot_rows = nc.dram_tensor("slot_rows", [ROWS, P], F32, kind="Internal").ap()
        expert_rows = nc.dram_tensor("expert_rows", [E * SLOTS, P], F32, kind="Internal").ap()

        consts_made = sem("consts_made")
        mix_weights_in = sem("mix_weights_in")
        small_in = sem("small_in")
        expert_weights_in = [sem(f"expert_weights_in{e}") for e in range(E)]
        bproj_in = sem("bproj_in")
        x_loaded = sem("x_loaded")
        weights_turned = sem("weights_turned")
        weights_copied = sem("weights_copied")
        stats_made = sem("stats_made")
        moments_made = sem("moments_made")
        shifted_made = sem("shifted_made")
        rstd_made = sem("rstd_made")
        normed_made = sem("normed_made")
        turned_ps = sem("turned_ps")
        turned_sb = sem("turned_sb")
        k_made = sem("k_made")
        v_made = sem("v_made")
        r_made = sem("r_made")
        k_copied = sem("k_copied")
        r_copied = sem("r_copied")
        kv_made = sem("kv_made")
        state_made = sem("state_made")
        mixed_made = sem("mixed_made")
        out_made = sem("out_made")
        x_added = sem("x_added")
        skip_made = sem("skip_made")
        logits_made = sem("logits_made")
        logits_copied = sem("logits_copied")
        top_made = sem("top_made")
        top_index_made = sem("top_index_made")
        top_copied = sem("top_copied")
        chosen_made = sem("chosen_made")
        gap_made = sem("gap_made")
        gap_turned = sem("gap_turned")
        counts_made = sem("counts_made")
        rows_step = sem("rows_step")
        rows_made = sem("rows_made")
        rows_reduced = sem("rows_reduced")
        vector_consts = sem("vector_consts")
        pool_consts = sem("pool_consts")
        share_made = sem("share_made")
        kept = sem("kept")
        zeroed = sem("zeroed")
        rows_zeroed = sem("rows_zeroed")
        scattered = sem("scattered")
        slots_loaded = [sem(f"slots_loaded{g}") for g in range(GROUPS)]
        slots_turned = sem("slots_turned")
        slots_copied = sem("slots_copied")
        g_made = sem("g_made")
        h_made = sem("h_made")
        g_copied = sem("g_copied")
        prod_made = sem("prod_made")
        hidden_made = sem("hidden_made")
        o_made = sem("o_made")
        o_copied = sem("o_copied")
        o_stored = sem("o_stored")
        gathered = [sem(f"gathered{i}") for i in range(2)]
        part_made = sem("part_made")
        y_made = sem("y_made")
        y_stats_made = sem("y_stats_made")
        y_moments_made = sem("y_moments_made")
        y_shifted_made = sem("y_shifted_made")
        y_rstd_made = sem("y_rstd_made")
        y_normed = sem("y_normed")
        out_stored = sem("out_stored")

        h_view = h.rearrange("b (j p) d -> b p j d", p=P)
        out_view = out.rearrange("b (j p) d -> b p j d", p=P)
        slot_view = slot_rows.rearrange("(g j p) d -> g p j d", p=P, j=4)
        expert_view = expert_rows.rearrange("(e i p) d -> e p i d", i=PARTS, p=PART)

        block = ctx.enter_context(nc.Block())

        @block.sync
        def _(sp):
            def load_x(b):
                if later(b):
                    sp.wait_ge(skip_made, b)
                    sp.wait_ge(x_added, nth(b - 1, 4, 4))
                sp.dma_start(x_in[:, :, :], h_view[b]).then_inc(x_loaded, 16)

            def load_slots(b):
                sp.wait_ge(scattered, nth(b, 16 * TILES * K, 16 * TILES * K))
                if later(b):
                    sp.wait_ge(slots_turned, nth(b - 1, GROUPS, GROUPS))
                else:
                    sp.wait_ge(rows_zeroed, 16 * GROUPS)
                for g in range(GROUPS):
                    sp.dma_start(slot_x[:, 4 * g:4 * g + 4, :], slot_view[g]).then_inc(slots_loaded[g], 16)

            def store_expert(b, e):
                if e == 0 and later(b):
                    for i in range(2):
                        sp.wait_ge(gathered[i], nth(b - 1, 16 * TILES, 16 * TILES))
                sp.wait_ge(o_copied, nth(b, E, e + 1))
                sp.dma_start(expert_view[e], o_sb[:, e, :, :]).then_inc(o_stored, 16)

            def store_out(b):
                for i in range(2):
                    sp.wait_ge(y_normed, nth(b + 1, 2, i + 1))
                    sp.dma_start(out_view[b][:, HT * i:HT * i + HT, :],
                                 y_out[:, HT * i:HT * i + HT, :]).then_inc(out_stored, 16)

            def sequence(b, mix, combine):
                for e in range(E):
                    if e == E - 2 and mix:
                        load_slots(b + 1)
                    store_expert(b, e)
                    if e == 3 and combine:
                        store_out(b - 1)
                    if e == 4 and mix == "more":
                        load_x(b + 2)

            load_x(0)
            for i, w in enumerate((Wk, Wv, Wr, Wo)):
                sp.dma_start(w_raw[:, L * i:L * i + L, :], w.rearrange("l e d -> e l d")).then_inc(mix_weights_in, 16)
            with nc.allow_non_contiguous_dma("per-feature columns"):
                sp.dma_start(lnw_sb[:, :], ln_w.rearrange("l d -> d l")).then_inc(small_in, 16)
                sp.dma_start(lnb_sb[:, :], ln_b.rearrange("l d -> d l")).then_inc(small_in, 16)
                sp.dma_start(bfc_sb[:, :, :], b_fc.rearrange("e a (c p) -> p e (a c)", p=P)).then_inc(small_in, 16)
                sp.dma_start(bgate_sb[:, :, :], b_gate.rearrange("e a (c p) -> p e (a c)", p=P)).then_inc(small_in, 16)
            sp.dma_start(router_sb[:, :], router_w).then_inc(small_in, 16)
            sp.dma_start(rbias_sb[:, :], router_b.partition_broadcast(P)).then_inc(small_in, 16)
            sp.wait_ge(zeroed, 1)
            for g in range(GROUPS):
                sp.dma_start(slot_view[g], slot_x[:, 4 * g:4 * g + 4, :]).then_inc(rows_zeroed, 16)
            sp.dma_start(bproj_sb[:, :, :], b_proj.rearrange("e a d -> (e a d)").partition_broadcast(P))\
              .then_inc(bproj_in, 16)
            for e in range(E):
                sp.dma_start(gate_sb[:, e, :], w_gate[e]).then_inc(expert_weights_in[e], 16)
                sp.dma_start(fc_sb[:, e, :], w_fc[e]).then_inc(expert_weights_in[e], 16)
                sp.dma_start(proj_sb[:, e, :, :], w_proj[e].rearrange("(c p) d -> p c d", p=P))\
                  .then_inc(expert_weights_in[e], 16)
            load_x(1)
            load_slots(0)
            sequence(0, "more", False)
            with sp.Fori(1, B - 2) as b:
                sequence(b, "more", True)
            sequence(B - 2, "last", True)
            sequence(B - 1, None, True)
            store_out(B - 1)
            sp.wait_ge(out_stored, nth(B, 32, 32))

        @block.tensor
        def _(pe):
            def turn(b, n):
                pe.wait_ge(normed_made, nth(b, 6, n + 1))
                if n > 0:
                    if n <= 4:
                        pe.wait_ge(r_copied, nth(b, 4, n))
                    else:
                        pe.wait_ge(turned_sb, nth(b, 6, n))
                elif later(b):
                    pe.wait_ge(slots_copied, nth(b - 1, GROUPS, GROUPS))
                source = normed if n < 4 else x_ln
                for j in range(HT):
                    mm = nc.tensor.transpose(bank[0][:, P * j:P * j + P], source[:, HT * (n % 2) + j, :], ident[:, :])
                mm.then_inc(turned_ps, 1)

            def kvr(b, n):
                half = slice(HALF * (n % 2), HALF * (n % 2) + HALF)
                layer = n // 2
                pe.wait_ge(turned_sb, nth(b, 6, n + 1))
                if n % 2:
                    pe.wait_ge(k_copied, nth(b, 4, n))
                elif n:
                    pe.wait_ge(x_added, nth(b, 4, n - 1))
                nc.tensor.matmul(bank[1][:, :], w_mix[:, layer, :], normT[:, half], start=True, stop=True)\
                  .then_inc(k_made, 1)
                if n % 2:
                    pe.wait_ge(kv_made, nth(b, 4, n))
                elif n:
                    pe.wait_ge(x_added, nth(b, 4, n))
                nc.tensor.matmul(bank[2][:, :], w_mix[:, L + layer, :], normT[:, half], start=True, stop=True)\
                  .then_inc(v_made, 1)
                nc.tensor.matmul(bank[0][:, :], w_mix[:, 2 * L + layer, :], normT[:, half], start=True, stop=True)\
                  .then_inc(r_made, 1)

            def out(b, n):
                half = n % 2
                pe.wait_ge(mixed_made, nth(b, 4, n + 1))
                if half == 0:
                    pe.wait_ge(k_copied, nth(b, 4, n + 2))
                else:
                    pe.wait_ge(kv_made, nth(b, 4, n + 1))
                for j in range(HT):
                    mm = nc.tensor.matmul(bank[1 + half][:, P * j:P * j + P],
                                          mixed[:, HALF * half + P * j:HALF * half + P * j + P],
                                          w_mix[:, 3 * L + n // 2, :], start=True, stop=True)
                mm.then_inc(out_made, 1)

            def logits(b, half):
                pe.wait_ge(turned_sb, nth(b, 6, 5 + half))
                if half == 0:
                    pe.wait_ge(x_added, nth(b, 4, 4))
                else:
                    pe.wait_ge(logits_copied, nth(b, 2, 1))
                for j in range(HT):
                    mm = nc.tensor.matmul(bank[2][:, E * j:E * j + E],
                                          normT[:, HALF * half + P * j:HALF * half + P * j + P],
                                          router_sb[:, :], start=True, stop=True)
                mm.then_inc(logits_made, 1)

            def count(b, _):
                pe.wait_ge(chosen_made, nth(b, 1, 1))
                pe.wait_ge(x_added, nth(b, 4, 3))
                counts = bank[1][:, 0:TILES * K * E].rearrange("p (j k e) -> p j k e", k=K, e=E)
                nc.tensor.matmul(bank[1][:, 0:TILES * K * E], upto[:, :],
                                 chosen[:, :, :, :].rearrange("p j k e -> p (j k e)"),
                                 start=True, stop=False, skip_group_check=True)
                for j in range(TILES - 1):
                    rest = TILES - 1 - j
                    for k in range(K):
                        nc.tensor.matmul(counts[:, j + 1:TILES, k, :], ones[:, :],
                                         chosen[:, j:j + 1, k, :].to_broadcast([P, rest, E]),
                                         start=False, stop=False, skip_group_check=True)
                for j in range(TILES):
                    mm = nc.tensor.matmul(counts[:, :, 1, :], ones[:, :],
                                          chosen[:, j:j + 1, 0, :].to_broadcast([P, TILES, E]),
                                          start=False, stop=(j == TILES - 1), skip_group_check=True)
                mm.then_inc(counts_made, 1)

            stages = {"turn": turn, "kvr": kvr, "out": out, "logits": logits, "count": count}

            def turn_slots(b, g):
                pe.wait_ge(slots_loaded[g], nth(b, 16, 16))
                if g >= 3:
                    pe.wait_ge(slots_copied, nth(b, GROUPS, g - 2))
                elif g == 0:
                    pe.wait_ge(turned_sb, nth(b, 6, 6))
                elif g == 1:
                    pe.wait_ge(rows_made, nth(b, 1, 1))
                else:
                    pe.wait_ge(logits_copied, nth(b, 2, 2))
                for j in range(4):
                    mm = nc.tensor.transpose(bank[g % 3][:, P * j:P * j + P], slot_x[:, 4 * g + j, :], ident[:, :])
                mm.then_inc(slots_turned, 1)

            def hidden_pair(b, e, j):
                c = e * HC + j
                cols = slice(e * SLOTS, e * SLOTS + COLS)
                if j == 0:
                    pe.wait_ge(slots_copied, nth(b, GROUPS, (e * SLOTS + COLS - 1) // (4 * P) + 1))
                    if not later(b):
                        pe.wait_ge(expert_weights_in[e], 48)
                if c >= 2 or later(b):
                    pe.wait_ge(prod_made, nth(b, POINTS, c - 1))
                nc.tensor.matmul(pair[c % 2][0][:, 0:COLS], gate_sb[:, e, P * j:P * j + P], slotT[:, cols],
                                 start=True, stop=True).then_inc(g_made, 1)
                nc.tensor.matmul(pair[c % 2][1][:, 0:COLS], fc_sb[:, e, P * j:P * j + P], slotT[:, cols],
                                 start=True, stop=True).then_inc(h_made, 1)

            def project(b, e):
                pe.wait_ge(hidden_made, nth(b, 2 * E, 2 * e + 2))
                if e or later(b):
                    pe.wait_ge(o_copied, nth(b, E, e))
                for i in range(PARTS):
                    for c in range(HC):
                        mm = nc.tensor.matmul(ps_o[0:PART, P * i:P * i + P],
                                              hidden[:, e % 2, c, PART * i:PART * i + PART], proj_sb[:, e, c, :],
                                              start=(c == 0), stop=(c == HC - 1))
                mm.then_inc(o_made, 1)

            def sequence(b, mix):
                for e in range(E):
                    for j in range(HC):
                        point = e * HC + j
                        hidden_pair(b, e, j)
                        if point < 2:
                            turn_slots(b, 3 + point)
                        if mix:
                            for name, n in TENSOR_STAGES.get(point, ()):
                                stages[name](b + 1, n)
                        if j == 2 and e > 0:
                            project(b, e - 1)
                project(b, E - 1)
                if mix:
                    for g in range(3):
                        turn_slots(b + 1, g)

            pe.wait_ge(consts_made, 6)
            pe.wait_ge(mix_weights_in, 16 * 4)
            for i in range(4 * L):
                mm = nc.tensor.transpose(bank[i // 4][:, P * (i % 4):P * (i % 4) + P], w_raw[:, i, :], ident[:, :])
            mm.then_inc(weights_turned, 1)
            pe.wait_ge(weights_copied, 2)
            pe.wait_ge(small_in, 16 * 6)
            for point in sorted(TENSOR_STAGES):
                for name, n in TENSOR_STAGES[point]:
                    stages[name](0, n)
            for g in range(3):
                turn_slots(0, g)
            sequence(0, True)
            with pe.Fori(1, B - 1) as b:
                sequence(b, True)
            sequence(B - 1, False)

        @block.scalar
        def _(act):
            def turned(b, n):
                act.wait_ge(turned_ps, nth(b, 6, n + 1))
                half = n % 2
                if n >= 2 and n < 4:
                    act.wait_ge(r_made, nth(b, 4, n - 1))
                elif n >= 4:
                    act.wait_ge(r_made, nth(b, 4, n - 1))
                elif later(b):
                    act.wait_ge(logits_made, nth(b - 1, 2, half + 1))
                dst = normT[:, HALF * half:HALF * half + HALF]
                if n < 4:
                    nc.scalar.activation(dst, bank[0][:, :], ACT.Identity, bias=lnb_sb[:, n // 2:n // 2 + 1],
                                         scale=lnw_sb[:, n // 2:n // 2 + 1]).then_inc(turned_sb, 1)
                else:
                    nc.scalar.activation(dst, bank[0][:, :], ACT.Copy).then_inc(turned_sb, 1)

            def kr(b, n):
                half = slice(HALF * (n % 2), HALF * (n % 2) + HALF)
                act.wait_ge(k_made, nth(b, 4, n + 1))
                if n >= 2 or later(b):
                    act.wait_ge(kv_made, nth(b, 4, n - 1))
                nc.scalar.activation(k_sb[:, half], bank[1][:, :], ACT.Copy, scale=(1.0 - DECAY) / 2)\
                  .then_inc(k_copied, 1)
                act.wait_ge(r_made, nth(b, 4, n + 1))
                if n >= 2 or later(b):
                    act.wait_ge(mixed_made, nth(b, 4, n - 1))
                nc.scalar.activation(gate_r[:, half], bank[0][:, :], ACT.Tanh, scale=0.5).then_inc(r_copied, 1)

            def lead(b, _):
                act.wait_ge(gap_made, nth(b, 1, 1))
                if later(b):
                    act.wait_ge(share_made, nth(b - 1, 1, 1))
                nc.scalar.activation(gap_t[:, :], gap[:, :], ACT.Tanh, scale=0.5).then_inc(gap_turned, 1)

            stages = {"turned": turned, "kr": kr, "lead": lead}

            def copy_slots(b, g):
                act.wait_ge(slots_turned, nth(b, GROUPS, g + 1))
                if later(b):
                    act.wait_ge(h_made, nth(b - 1, POINTS, POINTS))
                nc.scalar.activation(slotT[:, 4 * P * g:4 * P * g + 4 * P], bank[g % 3][:, :], ACT.Copy)\
                  .then_inc(slots_copied, 1)

            def gate_copy(b, e, j):
                c = e * HC + j
                act.wait_ge(g_made, nth(b, POINTS, c + 1))
                if c >= 2 or later(b):
                    act.wait_ge(prod_made, nth(b, POINTS, c - 1))
                nc.scalar.activation(gate_s[:, c % 2, :], pair[c % 2][0][:, 0:COLS], ACT.Identity,
                                     bias=bgate_sb[:, e, j:j + 1]).then_inc(g_copied, 1)

            def silu(b, e, i):
                act.wait_ge(prod_made, nth(b, POINTS, e * HC + 2 * i + 2))
                if e >= 2 or later(b):
                    act.wait_ge(o_made, nth(b, E, e - 1))
                nc.scalar.activation(hidden[:, e % 2, 2 * i:2 * i + 2, 0:COLS], prod[:, e % 2, 2 * i:2 * i + 2, :],
                                     ACT.Silu).then_inc(hidden_made, 1)

            def sequence(b, mix):
                for e in range(E):
                    for j in range(HC):
                        point = e * HC + j
                        gate_copy(b, e, j)
                        if point < 2:
                            copy_slots(b, 3 + point)
                        if mix:
                            for name, n in SCALAR_STAGES.get(point, ()):
                                stages[name](b + 1, n)
                        if j == 1 and e > 0:
                            silu(b, e - 1, 1)
                        if j == 3:
                            silu(b, e, 0)
                silu(b, E - 1, 1)
                if mix:
                    for g in range(3):
                        copy_slots(b + 1, g)

            act.wait_ge(small_in, 16 * 6)
            act.wait_ge(weights_turned, 1)
            for i in range(2):
                nc.scalar.activation(w_mix[:, 4 * i:4 * i + 4, :],
                                     bank[i][:, :].rearrange("p (w d) -> p w d", w=4), ACT.Copy)\
                  .then_inc(weights_copied, 1)
            for point in sorted(SCALAR_STAGES):
                for name, n in SCALAR_STAGES[point]:
                    stages[name](0, n)
            for g in range(3):
                copy_slots(0, g)
            sequence(0, True)
            with act.Fori(1, B - 1) as b:
                sequence(b, True)
            sequence(B - 1, False)

        @block.vector
        def _(dve):
            def stats_of(b, n):
                norm, half = divmod(n, 2)
                source = (x_in, x_mid, x_sum)[norm]
                if norm == 0 and half == 0:
                    dve.wait_ge(x_loaded, nth(b, 16, 16))
                if norm > 0:
                    dve.wait_ge(x_added, nth(b, 4, n - 1))
                if later(b):
                    dve.wait_ge(normed_made, nth(b - 1, 6, n + 1))
                for j in range(HT * half, HT * half + HT):
                    i = nc.vector.bn_stats(stats[:, norm, j, :], source[:, j, :])
                i.then_inc(stats_made, 1)
                ahead(dve, nth(b, 6, n + 1))
                dve.wait_ge(vector_consts, 2)
                dve.wait_ge(stats_made, nth(b, 6, n + 1))
                for j in range(HT * half, HT * half + HT):
                    i = nc.vector.bn_aggr(moments[:, norm, j, :], stats[:, norm, j, :])
                i.then_inc(moments_made, 1)

            def norm_of(b, n):
                norm, half = divmod(n, 2)
                source = (x_in, x_mid, x_sum)[norm]
                dve.wait_ge(rstd_made, nth(b, 6, n + 1))
                if norm == 0 and later(b):
                    dve.wait_ge(turned_ps, nth(b - 1, 6, 3 + half))
                elif norm == 1:
                    dve.wait_ge(turned_ps, nth(b, 6, 1 + half))
                elif norm == 2 and later(b):
                    dve.wait_ge(scattered, nth(b - 1, 16 * TILES * K, 16 * TILES * K))
                    dve.wait_ge(kept, nth(b - 1, 3, 3))
                dve.wait_ge(moments_made, nth(b, 6, n + 1))
                dst = normed if norm < 2 else x_ln
                for j in range(HT * half, HT * half + HT):
                    i = nc.vector.tensor_scalar(dst[:, j, :], source[:, j, :], moments[:, norm, j, 0:1],
                                                rstd[:, norm, j:j + 1], ALU.subtract, ALU.mult)
                i.then_inc(normed_made, 1)

            def mix(b, n):
                lo, hi = HALF * (n % 2), HALF * (n % 2) + HALF
                dve.wait_ge(k_copied, nth(b, 4, n + 1))
                dve.wait_ge(v_made, nth(b, 4, n + 1))
                if n >= 2 or later(b):
                    dve.wait_ge(state_made, nth(b, 4, n - 1))
                nc.vector.tensor_tensor(kv_sb[:, lo:hi], bank[2][:, :], k_sb[:, lo:hi], ALU.mult).then_inc(kv_made, 1)
                dve.wait_ge(kv_made, nth(b, 4, n + 1))
                if n >= 2 or later(b):
                    dve.wait_ge(mixed_made, nth(b, 4, n - 1))
                if n % 2:
                    dve.wait_ge(state_made, nth(b, 4, n))
                nc.vector.tensor_tensor_scan(state[:, lo:hi], decay[:, :], kv_sb[:, lo:hi],
                                             state[:, lo - 1:lo] if n % 2 else 0.0, ALU.mult, ALU.add)\
                  .then_inc(state_made, 1)
                dve.wait_ge(r_copied, nth(b, 4, n + 1))
                dve.wait_ge(state_made, nth(b, 4, n + 1))
                if n >= 2 or later(b):
                    dve.wait_ge(out_made, nth(b, 4, n - 1))
                nc.vector.scalar_tensor_tensor(mixed[:, lo:hi], gate_r[:, lo:hi], 1.0, state[:, lo:hi],
                                               ALU.add, ALU.mult).then_inc(mixed_made, 1)

            def add(b, n):
                layer, half = divmod(n, 2)
                tiles = slice(HT * half, HT * half + HT)
                dve.wait_ge(out_made, nth(b, 4, n + 1))
                if layer == 0:
                    if later(b):
                        dve.wait_ge(skip_made, nth(b - 1, 1, 1))
                        dve.wait_ge(normed_made, nth(b - 1, 6, 3 + half))
                    src, dst = x_in, x_mid
                else:
                    dve.wait_ge(skip_made, nth(b, 1, 1))
                    if later(b):
                        dve.wait_ge(normed_made, nth(b - 1, 6, 5 + half))
                    src, dst = x_skip, x_sum
                nc.vector.tensor_tensor(dst[:, tiles, :], src[:, tiles, :],
                                        bank[1 + half][:, :].rearrange("p (j d) -> p j d", d=P), ALU.add)\
                  .then_inc(x_added, 1)

            def top(b, half):
                tiles = range(HT * half, HT * half + HT)
                dve.wait_ge(logits_made, nth(b, 2, half + 1))
                if later(b):
                    dve.wait_ge(top_index_made, nth(b - 1, 2, half + 1))
                nc.vector.tensor_tensor(logit[:, HT * half:HT * half + HT, :],
                                        bank[2][:, 0:HT * E].rearrange("p (j e) -> p j e", e=E),
                                        rbias_sb[:, :].rearrange("p (o e) -> p o e", o=1).to_broadcast([P, HT, E]),
                                        ALU.add).then_inc(logits_copied, 1)
                ahead(dve, nth(b, 2, half + 1), nth(b - 1, 1, 1))
                dve.wait_ge(vector_consts, 2)
                dve.wait_ge(logits_copied, nth(b, 2, half + 1))
                if later(b):
                    dve.wait_ge(gap_made, nth(b - 1, 1, 1))
                for j in tiles:
                    i = nc.vector.max(top_v[:, j, :], logit[:, j, :])
                i.then_inc(top_made, 1)
                ahead(dve, nth(b, 2, half + 1), nth(b - 1, 1, 1))
                dve.wait_ge(vector_consts, 2)
                dve.wait_ge(top_made, nth(b, 2, half + 1))
                if later(b):
                    dve.wait_ge(top_copied, nth(b - 1, 1, 1))
                for j in tiles:
                    i = nc.vector.max_index(top_i[:, j, :], top_v[:, j, :], logit[:, j, :])
                i.then_inc(top_index_made, 1)

            def choice(b, _):
                dve.wait_ge(top_made, nth(b, 2, 2))
                if later(b):
                    dve.wait_ge(gap_turned, nth(b - 1, 1, 1))
                nc.vector.tensor_tensor(gap[:, :], top_v[:, :, 0:1].rearrange("p j o -> p (j o)"),
                                        top_v[:, :, 1:2].rearrange("p j o -> p (j o)"), ALU.subtract)\
                  .then_inc(gap_made, 1)
                dve.wait_ge(top_index_made, nth(b, 2, 2))
                if later(b):
                    dve.wait_ge(chosen_made, nth(b - 1, 1, 1))
                nc.vector.tensor_copy(top_f[:, :, :], top_i[:, :, 0:K]).then_inc(top_copied, 1)
                dve.wait_ge(top_copied, nth(b, 1, 1))
                if later(b):
                    dve.wait_ge(rows_made, nth(b - 1, 1, 1))
                nc.vector.tensor_tensor(
                    chosen[:, :, :, :].rearrange("p j k e -> p (j k) e"),
                    expert_id[:, :].rearrange("p (c e) -> p c e", e=E),
                    top_f[:, :, :].rearrange("p j (k o) -> p (j k) o", o=1).to_broadcast([P, TILES * K, E]),
                    ALU.is_equal).then_inc(chosen_made, 1)

            def rows(b, _):
                counts = bank[1][:, 0:TILES * K * E]
                picks = chosen[:, :, :, :].rearrange("p j k e -> p (j k) e")
                dve.wait_ge(counts_made, nth(b, 1, 1))
                dve.wait_ge(chosen_made, nth(b, 1, 1))
                nc.vector.scalar_tensor_tensor(row_in[:, :], counts, float(CAP), expert_base[:, :],
                                               ALU.min, ALU.add).then_inc(rows_step, 1)
                nc.vector.tensor_scalar(row_far[:, :], counts, float(CAP), FAR, ALU.is_gt, ALU.mult)\
                  .then_inc(rows_step, 1)
                dve.wait_ge(rows_step, nth(b, 5, 2))
                nc.vector.tensor_tensor(row_both[:, 0, :, :], row_in[:, :].rearrange("p (c e) -> p c e", e=E),
                                        picks, ALU.mult).then_inc(rows_step, 1)
                nc.vector.tensor_tensor(row_far[:, :], row_far[:, :], row_in[:, :], ALU.add).then_inc(rows_step, 1)
                dve.wait_ge(rows_step, nth(b, 5, 4))
                nc.vector.tensor_tensor(row_both[:, 1, :, :], row_far[:, :].rearrange("p (c e) -> p c e", e=E),
                                        picks, ALU.mult).then_inc(rows_step, 1)
                dve.wait_ge(rows_step, nth(b, 5, 5))
                nc.vector.tensor_reduce(row_f[:, :, :].rearrange("p w c -> p (w c)"),
                                        row_both[:, :, :, :].rearrange("p w c e -> p (w c) e"), AX.X, ALU.add)\
                  .then_inc(rows_reduced, 1)
                dve.wait_ge(rows_reduced, nth(b, 1, 1))
                if later(b):
                    dve.wait_ge(kept, nth(b - 1, 3, 3))
                    dve.wait_ge(scattered, nth(b - 1, 16 * TILES * K, 16 * TILES * K))
                nc.vector.tensor_copy(row_from[:, :], row_f[:, 0, :])
                nc.vector.tensor_copy(row_to[:, :], row_f[:, 1, :]).then_inc(rows_made, 1)

            stages = {"stats": stats_of, "norm": norm_of, "mix": mix, "add": add, "top": top,
                      "choice": choice, "rows": rows}

            def gather_sum(b, half):
                dve.wait_ge(gathered[half], nth(b, 16 * TILES, 16 * TILES))
                if half == 0:
                    dve.wait_ge(kept, nth(b, 3, 3))
                if later(b):
                    dve.wait_ge(y_made, nth(b, 2, 2))
                for j in range(HT * half, HT * half + HT):
                    i = nc.vector.scalar_tensor_tensor(part_sum[:, j, :], picked[:, j, 0, :], share_old[:, j, 0:1],
                                                       x_old[:, j, :], ALU.mult, ALU.add)
                i.then_inc(part_made, 1)
                dve.wait_ge(part_made, nth(b, 2, half + 1))
                if later(b):
                    dve.wait_ge(y_normed, nth(b, 2, 2))
                for j in range(HT * half, HT * half + HT):
                    i = nc.vector.scalar_tensor_tensor(y_sum[:, j, :], picked[:, j, 1, :], share_old[:, j, 1:2],
                                                       part_sum[:, j, :], ALU.mult, ALU.add)
                i.then_inc(y_made, 1)
                dve.wait_ge(y_made, nth(b + 1, 2, half + 1))
                for j in range(HT * half, HT * half + HT):
                    i = nc.vector.bn_stats(y_stats[:, j, :], y_sum[:, j, :])
                i.then_inc(y_stats_made, 1)
                ahead(dve, nth(b, 2, half + 1))
                dve.wait_ge(vector_consts, 2)
                dve.wait_ge(y_stats_made, nth(b, 2, half + 1))
                for j in range(HT * half, HT * half + HT):
                    i = nc.vector.bn_aggr(y_moments[:, j, :], y_stats[:, j, :])
                i.then_inc(y_moments_made, 1)

            def final_norm(b, half):
                dve.wait_ge(y_rstd_made, nth(b, 2, half + 1))
                dve.wait_ge(y_moments_made, nth(b, 2, half + 1))
                if later(b):
                    dve.wait_ge(out_stored, nth(b, 32, 32))
                for j in range(HT * half, HT * half + HT):
                    i = nc.vector.tensor_scalar(y_out[:, j, :], y_sum[:, j, :], y_moments[:, j, 0:1],
                                                y_rstd[:, j:j + 1], ALU.subtract, ALU.mult)
                i.then_inc(y_normed, 1)

            combine_stages = {"gather_sum": gather_sum, "final_norm": final_norm}

            def product(b, e, j):
                c = e * HC + j
                dve.wait_ge(h_made, nth(b, POINTS, c + 1))
                dve.wait_ge(g_copied, nth(b, POINTS, c + 1))
                if j == 0 and (e >= 2 or later(b)):
                    dve.wait_ge(hidden_made, nth(b, 2 * E, 2 * e - 2))
                nc.vector.scalar_tensor_tensor(prod[:, e % 2, j, :], pair[c % 2][1][:, 0:COLS], bfc_sb[:, e, j:j + 1],
                                               gate_s[:, c % 2, :], ALU.add, ALU.mult).then_inc(prod_made, 1)

            def copy_out(b, e):
                dve.wait_ge(o_made, nth(b, E, e + 1))
                if later(b):
                    dve.wait_ge(o_stored, nth(b - 1, 16 * E, 16 * E))
                nc.vector.tensor_tensor(o_sb[:, e, :, :],
                                        ps_o[0:PART, 0:PARTS * P].rearrange("p (i d) -> p i d", d=P),
                                        bproj_sb[0:PART, e:e + 1, :].to_broadcast([PART, PARTS, P]), ALU.add)\
                  .then_inc(o_copied, 1)

            def sequence(b, mix, combine):
                for e in range(E):
                    for j in range(HC):
                        point = e * HC + j
                        product(b, e, j)
                        if combine:
                            for name, n in VECTOR_COMBINE.get(point, ()):
                                combine_stages[name](b - 1, n)
                        if mix:
                            for name, n in VECTOR_STAGES.get(point, ()):
                                stages[name](b + 1, n)
                        if j == 3 and e > 0:
                            copy_out(b, e - 1)
                copy_out(b, E - 1)

            nc.vector.memset(y_sum[:, 0, :], 0.0).then_inc(y_made, 2)
            nc.vector.memset(y_out[:, 0, :], 0.0).then_inc(y_normed, 2)
            nc.vector.memset(y_out[:, 1, :], 0.0).then_inc(out_stored, 32)
            nc.vector.memset(decay[:, :], DECAY).then_inc(vector_consts, 1)
            nc.vector.memset(hidden[:, :, :, :], 0.0).then_inc(vector_consts, 1)
            dve.wait_ge(vector_consts, 2)
            dve.wait_ge(consts_made, 6)
            dve.wait_ge(small_in, 16 * 6)
            for point in sorted(VECTOR_STAGES):
                for name, n in VECTOR_STAGES[point]:
                    stages[name](0, n)
            dve.wait_ge(bproj_in, 16)
            sequence(0, True, False)
            with dve.Fori(1, B - 1) as b:
                sequence(b, True, True)
            sequence(B - 1, False, True)
            for point in sorted(VECTOR_COMBINE):
                for name, n in VECTOR_COMBINE[point]:
                    combine_stages[name](B - 1, n)

        @block.gpsimd
        def _(pool):
            def rstd_of(b, n):
                norm, half = divmod(n, 2)
                tiles = slice(HT * half, HT * half + HT)
                ahead(pool, nth(b, 6, n + 1), nth(b - 1, 6, n + 1))
                pool.wait_ge(consts_made, 6)
                pool.wait_ge(moments_made, nth(b, 6, n + 1))
                if later(b):
                    pool.wait_ge(normed_made, nth(b - 1, 6, n + 1))
                nc.gpsimd.tensor_scalar(shifted[:, norm, tiles],
                                        moments[:, norm, tiles, 1:2].rearrange("p j o -> p (j o)"),
                                        EPS, None, ALU.add).then_inc(shifted_made, 1)
                pool.wait_ge(shifted_made, nth(b, 6, n + 1))
                nc.gpsimd.tensor_tensor(rstd[:, norm, tiles], shifted[:, norm, tiles], power[:, :], ALU.pow)\
                  .then_inc(rstd_made, 1)

            def skip_sum(b, _):
                pool.wait_ge(x_added, nth(b, 4, 2))
                pool.wait_ge(x_loaded, nth(b, 16, 16))
                if later(b):
                    pool.wait_ge(x_added, nth(b - 1, 4, 4))
                nc.gpsimd.tensor_tensor(x_skip[:, :, :], x_in[:, :, :], x_mid[:, :, :], ALU.add)\
                  .then_inc(skip_made, 1)

            def keep(b, _):
                ahead(pool, nth(b - 1, 2, 2), nth(b - 2, 16 * TILES, 16 * TILES), nth(b - 1, 6, 6))
                pool.wait_ge(consts_made, 6)
                if later(b - 1):
                    pool.wait_ge(y_made, nth(b - 1, 2, 2))
                    for i in range(2):
                        pool.wait_ge(gathered[i], nth(b - 2, 16 * TILES, 16 * TILES))
                pool.wait_ge(normed_made, nth(b - 1, 6, 6))
                nc.gpsimd.tensor_copy(x_old[:, :, :], x_ln[:, :, :]).then_inc(kept, 1)
                ahead(pool, nth(b - 1, 1, 1))
                pool.wait_ge(consts_made, 6)
                pool.wait_ge(rows_made, nth(b - 1, 1, 1))
                nc.gpsimd.tensor_copy(row_old[:, :], row_from[:, :]).then_inc(kept, 1)
                ahead(pool, nth(b - 1, 1, 1))
                pool.wait_ge(consts_made, 6)
                pool.wait_ge(share_made, nth(b - 1, 1, 1))
                nc.gpsimd.tensor_copy(share_old[:, :, :], share[:, :, :]).then_inc(kept, 1)

            def shares(b, _):
                ahead(pool, nth(b, 1, 1), nth(b - 1, 3, 3))
                pool.wait_ge(consts_made, 6)
                pool.wait_ge(gap_turned, nth(b, 1, 1))
                if later(b):
                    pool.wait_ge(kept, nth(b - 1, 3, 3))
                nc.gpsimd.tensor_scalar(share[:, :, 0:1].rearrange("p j o -> p (j o)"), gap_t[:, :], 0.5, 0.5,
                                        ALU.mult, ALU.add)
                nc.gpsimd.tensor_scalar(share[:, :, 1:2].rearrange("p j o -> p (j o)"), gap_t[:, :], -0.5, 0.5,
                                        ALU.mult, ALU.add).then_inc(share_made, 1)

            def scatter(b, _):
                ahead(pool, nth(b, 1, 1), nth(b, 6, 6), nth(b - 1, 16, 16))
                pool.wait_ge(consts_made, 6)
                pool.wait_ge(rows_made, nth(b, 1, 1))
                pool.wait_ge(normed_made, nth(b, 6, 6))
                if later(b):
                    for g in range(GROUPS):
                        pool.wait_ge(slots_loaded[g], nth(b - 1, 16, 16))
                else:
                    pool.wait_ge(rows_zeroed, 16 * GROUPS)
                for j in range(TILES):
                    for k in range(K):
                        c = j * K + k
                        nc.gpsimd.indirect_dma_start(
                            out=slot_rows, out_offset=bass.IndirectOffsetOnAxis(ap=row_to[:, c:c + 1], axis=0),
                            in_=x_ln[:, j, :], in_offset=None, bounds_check=ROWS - 1, oob_is_err=False)\
                          .then_inc(scattered, 16)

            stages = {"rstd": rstd_of, "skip_sum": skip_sum, "keep": keep, "shares": shares, "scatter": scatter}

            def gather(b, half):
                ahead(pool, nth(b, 16 * E, 16 * E), nth(b, 3, 3), nth(b, 2, 2))
                pool.wait_ge(consts_made, 6)
                if half == 0:
                    pool.wait_ge(o_stored, nth(b, 16 * E, 16 * E))
                    pool.wait_ge(kept, nth(b, 3, 3))
                if later(b):
                    pool.wait_ge(y_made, nth(b, 2, 2))
                for j in range(HT * half, HT * half + HT):
                    for k in range(K):
                        c = j * K + k
                        nc.gpsimd.indirect_dma_start(
                            out=picked[:, j, k, :], out_offset=None, in_=expert_rows,
                            in_offset=bass.IndirectOffsetOnAxis(ap=row_old[:, c:c + 1], axis=0),
                            bounds_check=E * SLOTS - 1, oob_is_err=False).then_inc(gathered[half], 16)

            def final_rstd(b, half):
                tiles = slice(HT * half, HT * half + HT)
                ahead(pool, nth(b, 2, half + 1), nth(b, 2, 2))
                pool.wait_ge(consts_made, 6)
                pool.wait_ge(y_moments_made, nth(b, 2, half + 1))
                if later(b):
                    pool.wait_ge(y_normed, nth(b, 2, 2))
                nc.gpsimd.tensor_scalar(y_shifted[:, tiles],
                                        y_moments[:, tiles, 1:2].rearrange("p j o -> p (j o)"),
                                        EPS, None, ALU.add).then_inc(y_shifted_made, 1)
                pool.wait_ge(y_shifted_made, nth(b, 2, half + 1))
                nc.gpsimd.tensor_tensor(y_rstd[:, tiles], y_shifted[:, tiles], power[:, :], ALU.pow)\
                  .then_inc(y_rstd_made, 1)

            combine_stages = {"gather": gather, "final_rstd": final_rstd}

            def sequence(b, mix, combine):
                for point in range(POINTS):
                    if combine:
                        for name, n in POOL_COMBINE.get(point, ()):
                            combine_stages[name](b - 1, n)
                    if mix:
                        for name, n in POOL_STAGES.get(point, ()):
                            stages[name](b + 1, n)

            nc.gpsimd.memset(slot_x[:, :, :], 0.0).then_inc(zeroed, 1)
            nc.gpsimd.memset(ident[:, :], 0.0).then_inc(pool_consts, 1)
            nc.gpsimd.memset(ones[:, :], 1.0).then_inc(consts_made, 1)
            nc.gpsimd.memset(power[:, :], -0.5).then_inc(consts_made, 1)
            nc.gpsimd.memset(upto[:, :], 1.0).then_inc(pool_consts, 1)
            pool.wait_ge(pool_consts, 2)
            nc.gpsimd.affine_select(out=ident[:, :], in_=ident[:, :], compare_op=ALU.not_equal, fill=1.0, base=0,
                                    pattern=[[-1, P]], channel_multiplier=1).then_inc(consts_made, 1)
            nc.gpsimd.affine_select(out=upto[:, :], in_=upto[:, :], compare_op=ALU.is_ge, fill=0.0, base=0,
                                    pattern=[[1, P]], channel_multiplier=-1).then_inc(consts_made, 1)
            nc.gpsimd.iota(expert_id[:, :], pattern=[[0, TILES * K], [1, E]], base=0, channel_multiplier=0,
                           allow_small_or_imprecise_dtypes=True).then_inc(consts_made, 1)
            nc.gpsimd.iota(expert_base[:, :], pattern=[[0, TILES * K], [SLOTS, E]], base=-1, channel_multiplier=0,
                           allow_small_or_imprecise_dtypes=True).then_inc(consts_made, 1)
            pool.wait_ge(consts_made, 6)
            for point in sorted(POOL_STAGES):
                for name, n in POOL_STAGES[point]:
                    if name != "keep":
                        stages[name](0, n)
            sequence(0, True, False)
            with pool.Fori(1, B - 1) as b:
                sequence(b, True, True)
            sequence(B - 1, False, True)
            keep(B, 0)
            for point in sorted(POOL_COMBINE):
                for name, n in POOL_COMBINE[point]:
                    combine_stages[name](B - 1, n)


_INPUTS = ["L0_attn_h", "L0_attn_ln_w", "L0_attn_ln_b", "L0_attn_Wk", "L0_attn_Wv", "L0_attn_Wr", "L0_attn_Wo",
           "L0_ffn_router_w", "L0_ffn_router_b", "L0_ffn_w_c_fc", "L0_ffn_b_c_fc", "L0_ffn_w_gate",
           "L0_ffn_b_gate", "L0_ffn_w_c_proj", "L0_ffn_b_c_proj"]


def kernel(**inputs):
    import concourse.bacc as bacc
    from concourse.bass_utils import run_bass_kernel_spmd

    nc = bacc.Bacc("TRN2", target_bir_lowering=False, num_devices=1)
    arrays, args = {}, []
    for name in _INPUTS:
        a = np.ascontiguousarray(inputs[name])
        arrays[f"in_{name}"] = a
        args.append(nc.dram_tensor(f"in_{name}", a.shape, mybir.dt.from_np(a.dtype), kind="ExternalInput").ap())
    args.append(nc.dram_tensor("out_0", (B, T, P), F32, kind="ExternalOutput").ap())
    time_mix_moe(nc, *args)
    r = run_bass_kernel_spmd(nc, [arrays], core_ids=[0])
    return r.results[0]["out_0"]
```

```python
from contextlib import ExitStack

import numpy as np
import concourse.bass as bass
from concourse import mybir

ALU = mybir.AluOpType
ACT = mybir.ActivationFunctionType
AX = mybir.AxisListType
F32 = mybir.dt.float32
BF16 = mybir.dt.bfloat16
U32 = mybir.dt.uint32

P = 128
B, T, L = 4, 1024, 2
TILES = T // P
HT = TILES // 2
HALF = HT * P
E, K, H = 8, 2, 512
HC = H // P
CAP = int(1.2 * K * T // E)
COLS = CAP + CAP % 2
PART = 104
PARTS = 3
SLOTS = PART * PARTS
GROUPS = -(-E * SLOTS // (4 * P))
ROWS = GROUPS * 4 * P
POINTS = E * HC
FAR = float(1 << 20)
EPS = 1e-5
DECAY = 0.95

assert CAP <= COLS <= SLOTS and L == 2 and K == 2

RING = 3

TENSOR_MIX = {8: [("turn", 0)], 9: [("kvr", 0)], 10: [("turn", 1)], 11: [("kvr", 1)], 12: [("out", 0)],
              13: [("out", 1)], 16: [("turn", 2)], 17: [("kvr", 2)], 18: [("turn", 3)], 19: [("kvr", 3)],
              20: [("out", 2)], 21: [("out", 3)]}
TENSOR_ROUTE = {2: [("turn", 4)], 3: [("logits", 0), ("turn", 5)], 4: [("logits", 1)], 6: [("count", 0)]}
SCALAR_MIX = {8: [("turned", 0)], 9: [("kr", 0)], 10: [("turned", 1)], 11: [("kr", 1)],
              16: [("turned", 2)], 17: [("kr", 2)], 18: [("turned", 3)], 19: [("kr", 3)]}
SCALAR_ROUTE = {2: [("turned", 4)], 3: [("turned", 5)], 5: [("lead", 0)]}
VECTOR_MIX = {5: [("stats", 0), ("stats", 1)], 7: [("norm", 0), ("norm", 1)], 10: [("mix", 0)], 12: [("mix", 1)],
              13: [("add", 0), ("stats", 2)], 14: [("add", 1), ("stats", 3)], 15: [("norm", 2), ("norm", 3)],
              18: [("mix", 2)], 20: [("mix", 3)], 21: [("add", 2), ("stats", 4)], 22: [("add", 3), ("stats", 5)]}
VECTOR_ROUTE = {0: [("norm", 4)], 1: [("norm", 5)], 3: [("top", 0)], 4: [("top", 1), ("choice", 0)], 6: [("rows", 0)]}
VECTOR_COMBINE = {6: [("gather_sum", 0)], 8: [("final_norm", 0)], 11: [("gather_sum", 1)], 13: [("final_norm", 1)]}
POOL_MIX = {6: [("rstd", 0), ("rstd", 1)], 14: [("rstd", 2), ("rstd", 3)], 17: [("skip_sum", 0)],
            22: [("rstd", 4), ("rstd", 5)]}
POOL_ROUTE = {5: [("shares", 0)], **{10 + j: [("scatter", j)] for j in range(8)}}
POOL_COMBINE = {**{1 + j: [("gather", j)] for j in range(8)}, 7: [("final_rstd", 0), ("gather", 6)],
                11: [("final_rstd", 1)]}


def nth(b, per, k):
    return b * per + k


def later(b):
    return b > 0


def time_mix_moe(nc, h, ln_w, ln_b, Wk, Wv, Wr, Wo, router_w, router_b, w_fc, b_fc, w_gate, b_gate,
                 w_proj, b_proj, out):
    with ExitStack() as ctx:
        def sb(name, shape, dt=F32):
            return ctx.enter_context(nc.sbuf_tensor(name, shape, dt))

        def sem(name):
            return ctx.enter_context(nc.semaphore(name))

        ident = sb("ident", [P, P])
        upto = sb("upto", [P, P], BF16)
        ones = sb("ones", [P, P], BF16)
        decay = sb("decay", [P, HALF])
        power = sb("power", [P, HT])
        expert_id = sb("expert_id", [P, TILES * K * E])
        expert_base = sb("expert_base", [P, TILES * K * E])
        lnw_sb = sb("lnw_sb", [P, L])
        lnb_sb = sb("lnb_sb", [P, L])
        w_raw = sb("w_raw", [P, 4 * L, P])
        w_mix = sb("w_mix", [P, 4 * L, P])
        router_sb = sb("router_sb", [P, E])
        rbias_sb = sb("rbias_sb", [P, E])
        fc_sb = sb("fc_sb", [P, E, H])
        gate_sb = sb("gate_sb", [P, E, H])
        proj_sb = sb("proj_sb", [P, E, HC, P])
        bfc_sb = sb("bfc_sb", [P, E, HC])
        bgate_sb = sb("bgate_sb", [P, E, HC])
        bproj_sb = sb("bproj_sb", [P, E, P])
        x_in = sb("x_in", [P, TILES, P])
        x_mid = sb("x_mid", [P, TILES, P])
        x_skip = sb("x_skip", [P, TILES, P])
        x_sum = sb("x_sum", [P, TILES, P])
        normed = sb("normed", [P, TILES, P])
        stats = sb("stats", [P, 3, TILES, 6])
        moments = sb("moments", [P, 3, TILES, 2])
        shifted = sb("shifted", [P, 3, TILES])
        rstd = sb("rstd", [P, 3, TILES])
        normT = sb("normT", [P, T])
        k_sb = sb("k_sb", [P, T])
        gate_r = sb("gate_r", [P, T])
        kv_sb = sb("kv_sb", [P, T])
        state = sb("state", [P, T])
        mixed = sb("mixed", [P, T])
        x_ln = sb("x_ln", [P, RING, TILES, P])
        logit = sb("logit", [P, TILES, E])
        top_v = sb("top_v", [P, TILES, 8])
        top_i = sb("top_i", [P, TILES, 8], U32)
        top_f = sb("top_f", [P, TILES, K])
        gap = sb("gap", [P, TILES])
        gap_t = sb("gap_t", [P, TILES])
        share = sb("share", [P, RING, TILES, K])
        chosen = sb("chosen", [P, TILES, K, E], BF16)
        row_in = sb("row_in", [P, TILES * K * E])
        row_far = sb("row_far", [P, TILES * K * E])
        row_both = sb("row_both", [P, 2, TILES * K, E])
        row_f = sb("row_f", [P, 2, TILES * K])
        row_to = sb("row_to", [P, TILES * K], U32)
        row_from = sb("row_from", [P, RING, TILES * K], U32)
        slot_x = sb("slot_x", [P, GROUPS * 4, P])
        slotT = sb("slotT", [P, ROWS])
        gate_s = sb("gate_s", [P, 2, COLS])
        prod = sb("prod", [P, 2, HC, COLS])
        hidden = sb("hidden", [P, 2, HC, SLOTS])
        o_sb = sb("o_sb", [PART, E, PARTS, P])
        picked = sb("picked", [P, TILES, K, P])
        part_sum = sb("part_sum", [P, TILES, P])
        y_sum = sb("y_sum", [P, TILES, P])
        y_out = sb("y_out", [P, TILES, P])
        y_stats = sb("y_stats", [P, TILES, 6])
        y_moments = sb("y_moments", [P, TILES, 2])
        y_shifted = sb("y_shifted", [P, TILES])
        y_rstd = sb("y_rstd", [P, TILES])

        pair = [[ctx.enter_context(nc.psum_tensor(f"pair{i}{n}", [P, 512], F32)) for n in "gh"] for i in range(2)]
        ps_o = ctx.enter_context(nc.psum_tensor("ps_o", [P, 512], F32))
        bank = [ctx.enter_context(nc.psum_tensor(f"bank{i}", [P, 512], F32)) for i in range(3)]

        slot_rows = nc.dram_tensor("slot_rows", [ROWS, P], F32, kind="Internal").ap()
        expert_rows = nc.dram_tensor("expert_rows", [E * SLOTS, P], F32, kind="Internal").ap()

        consts_made = sem("consts_made")
        mix_weights_in = sem("mix_weights_in")
        small_in = sem("small_in")
        expert_weights_in = [sem(f"expert_weights_in{e}") for e in range(E)]
        bproj_in = sem("bproj_in")
        x_loaded = sem("x_loaded")
        weights_turned = sem("weights_turned")
        weights_copied = sem("weights_copied")
        stats_made = sem("stats_made")
        moments_made = sem("moments_made")
        shifted_made = sem("shifted_made")
        rstd_made = sem("rstd_made")
        normed_made = sem("normed_made")
        turned_ps = sem("turned_ps")
        turned_sb = sem("turned_sb")
        k_made = sem("k_made")
        v_made = sem("v_made")
        r_made = sem("r_made")
        k_copied = sem("k_copied")
        r_copied = sem("r_copied")
        kv_made = sem("kv_made")
        state_made = sem("state_made")
        mixed_made = sem("mixed_made")
        out_made = sem("out_made")
        x_added = sem("x_added")
        skip_made = sem("skip_made")
        logits_made = sem("logits_made")
        logits_copied = sem("logits_copied")
        top_made = sem("top_made")
        top_index_made = sem("top_index_made")
        top_copied = sem("top_copied")
        chosen_made = sem("chosen_made")
        gap_made = sem("gap_made")
        gap_turned = sem("gap_turned")
        counts_made = sem("counts_made")
        rows_step = sem("rows_step")
        rows_made = sem("rows_made")
        rows_reduced = sem("rows_reduced")
        vector_consts = sem("vector_consts")
        pool_consts = sem("pool_consts")
        share_made = sem("share_made")
        zeroed = sem("zeroed")
        rows_zeroed = sem("rows_zeroed")
        scattered = sem("scattered")
        slots_loaded = [sem(f"slots_loaded{g}") for g in range(GROUPS)]
        slots_turned = sem("slots_turned")
        slots_copied = sem("slots_copied")
        g_made = sem("g_made")
        h_made = sem("h_made")
        g_copied = sem("g_copied")
        prod_made = sem("prod_made")
        hidden_made = sem("hidden_made")
        o_made = sem("o_made")
        o_copied = sem("o_copied")
        o_stored = sem("o_stored")
        gathered = [sem(f"gathered{i}") for i in range(2)]
        part_made = sem("part_made")
        y_made = sem("y_made")
        y_stats_made = sem("y_stats_made")
        y_moments_made = sem("y_moments_made")
        y_shifted_made = sem("y_shifted_made")
        y_rstd_made = sem("y_rstd_made")
        y_normed = sem("y_normed")
        out_stored = sem("out_stored")

        h_view = h.rearrange("b (j p) d -> b p j d", p=P)
        out_view = out.rearrange("b (j p) d -> b p j d", p=P)
        slot_view = slot_rows.rearrange("(g j p) d -> g p j d", p=P, j=4)
        expert_view = expert_rows.rearrange("(e i p) d -> e p i d", i=PARTS, p=PART)

        block = ctx.enter_context(nc.Block())

        @block.sync
        def _(sp):
            def load_x(b):
                if later(b):
                    sp.wait_ge(skip_made, nth(b - 1, 1, 1))
                sp.dma_start(x_in[:, :, :], h_view[b]).then_inc(x_loaded, 16)

            def load_slots(b):
                sp.wait_ge(scattered, nth(b, 16 * TILES * K, 16 * TILES * K))
                if later(b):
                    sp.wait_ge(slots_turned, nth(b - 1, GROUPS, GROUPS))
                else:
                    sp.wait_ge(rows_zeroed, 16 * GROUPS)
                for g in range(GROUPS):
                    sp.dma_start(slot_x[:, 4 * g:4 * g + 4, :], slot_view[g]).then_inc(slots_loaded[g], 16)

            def store_expert(b, e):
                if e == 0 and later(b):
                    for i in range(2):
                        sp.wait_ge(gathered[i], nth(b - 1, 16 * TILES, 16 * TILES))
                sp.wait_ge(o_copied, nth(b, E, e + 1))
                sp.dma_start(expert_view[e], o_sb[:, e, :, :]).then_inc(o_stored, 16)

            def store_out(b):
                for i in range(2):
                    sp.wait_ge(y_normed, nth(b, 2, i + 1))
                    sp.dma_start(out_view[b][:, HT * i:HT * i + HT, :],
                                 y_out[:, HT * i:HT * i + HT, :]).then_inc(out_stored, 16)

            def period(b):
                if 0 <= b + 2 < B - 1 and b < 0:
                    load_x(b + 3)
                if b == -1:
                    load_slots(0)
                for e in range(E if 0 <= b < B else 0):
                    store_expert(b, e)
                    if e == 2 and b > 0:
                        store_out(b - 1)
                    if e == 3 and b + 3 < B:
                        load_x(b + 3)
                    if e == 4 and b + 1 < B:
                        load_slots(b + 1)

            load_x(0)
            sp.wait_ge(zeroed, 1)
            for g in range(GROUPS):
                sp.dma_start(slot_view[g], slot_x[:, 4 * g:4 * g + 4, :]).then_inc(rows_zeroed, 16)
            for e in range(E):
                sp.dma_start(gate_sb[:, e, :], w_gate[e]).then_inc(expert_weights_in[e], 16)
                sp.dma_start(fc_sb[:, e, :], w_fc[e]).then_inc(expert_weights_in[e], 16)
                sp.dma_start(proj_sb[:, e, :, :], w_proj[e].rearrange("(c p) d -> p c d", p=P))\
                  .then_inc(expert_weights_in[e], 16)
            for b in range(-2, B):
                period(b)
            store_out(B - 1)
            sp.wait_ge(out_stored, nth(B, 32, 0))

        @block.tensor
        def _(pe):
            def turn(b, n):
                pe.wait_ge(normed_made, nth(b, 6, n + 1))
                if n == 0 and later(b):
                    pe.wait_ge(turned_sb, nth(b - 1, 6, 6))
                elif 0 < n < 5:
                    pe.wait_ge(r_copied, nth(b, 4, n))
                elif n == 5:
                    pe.wait_ge(turned_sb, nth(b, 6, n))
                if n == 4 and later(b):
                    pe.wait_ge(slots_copied, nth(b - 1, GROUPS, 4))
                source = normed if n < 4 else x_ln[:, b % RING, :, :]
                for j in range(HT):
                    mm = nc.tensor.transpose(bank[0][:, P * j:P * j + P], source[:, HT * (n % 2) + j, :], ident[:, :])
                mm.then_inc(turned_ps, 1)

            def kvr(b, n):
                half = slice(HALF * (n % 2), HALF * (n % 2) + HALF)
                layer = n // 2
                pe.wait_ge(turned_sb, nth(b, 6, n + 1))
                if n % 2:
                    pe.wait_ge(k_copied, nth(b, 4, n))
                elif n:
                    pe.wait_ge(x_added, nth(b, 4, n - 1))
                elif later(b):
                    pe.wait_ge(rows_made, nth(b - 1, 1, 1))
                nc.tensor.matmul(bank[1][:, :], w_mix[:, layer, :], normT[:, half], start=True, stop=True)\
                  .then_inc(k_made, 1)
                if n % 2:
                    pe.wait_ge(kv_made, nth(b, 4, n))
                elif n:
                    pe.wait_ge(x_added, nth(b, 4, n))
                elif later(b):
                    pe.wait_ge(logits_copied, nth(b - 1, 2, 2))
                nc.tensor.matmul(bank[2][:, :], w_mix[:, L + layer, :], normT[:, half], start=True, stop=True)\
                  .then_inc(v_made, 1)
                nc.tensor.matmul(bank[0][:, :], w_mix[:, 2 * L + layer, :], normT[:, half], start=True, stop=True)\
                  .then_inc(r_made, 1)

            def out(b, n):
                half = n % 2
                pe.wait_ge(mixed_made, nth(b, 4, n + 1))
                if half == 0:
                    pe.wait_ge(k_copied, nth(b, 4, n + 2))
                else:
                    pe.wait_ge(kv_made, nth(b, 4, n + 1))
                for j in range(HT):
                    mm = nc.tensor.matmul(bank[1 + half][:, P * j:P * j + P],
                                          mixed[:, HALF * half + P * j:HALF * half + P * j + P],
                                          w_mix[:, 3 * L + n // 2, :], start=True, stop=True)
                mm.then_inc(out_made, 1)

            def logits(b, half):
                pe.wait_ge(turned_sb, nth(b, 6, 5 + half))
                if half == 0:
                    pe.wait_ge(x_added, nth(b, 4, 4))
                    if later(b):
                        pe.wait_ge(slots_copied, nth(b - 1, GROUPS, 3))
                else:
                    pe.wait_ge(logits_copied, nth(b, 2, 1))
                for j in range(HT):
                    mm = nc.tensor.matmul(bank[2][:, E * j:E * j + E],
                                          normT[:, HALF * half + P * j:HALF * half + P * j + P],
                                          router_sb[:, :], start=True, stop=True)
                mm.then_inc(logits_made, 1)

            def count(b, _):
                pe.wait_ge(chosen_made, nth(b, 1, 1))
                pe.wait_ge(x_added, nth(b, 4, 3))
                if later(b):
                    pe.wait_ge(slots_copied, nth(b - 1, GROUPS, 5))
                counts = bank[1][:, 0:TILES * K * E].rearrange("p (j k e) -> p j k e", k=K, e=E)
                nc.tensor.matmul(bank[1][:, 0:TILES * K * E], upto[:, :],
                                 chosen[:, :, :, :].rearrange("p j k e -> p (j k e)"),
                                 start=True, stop=False, skip_group_check=True)
                for j in range(TILES - 1):
                    rest = TILES - 1 - j
                    for k in range(K):
                        nc.tensor.matmul(counts[:, j + 1:TILES, k, :], ones[:, :],
                                         chosen[:, j:j + 1, k, :].to_broadcast([P, rest, E]),
                                         start=False, stop=False, skip_group_check=True)
                for j in range(TILES):
                    mm = nc.tensor.matmul(counts[:, :, 1, :], ones[:, :],
                                          chosen[:, j:j + 1, 0, :].to_broadcast([P, TILES, E]),
                                          start=False, stop=(j == TILES - 1), skip_group_check=True)
                mm.then_inc(counts_made, 1)

            stages = {"turn": turn, "kvr": kvr, "out": out, "logits": logits, "count": count}

            def turn_slots(b, g):
                pe.wait_ge(slots_loaded[g], nth(b, 16, 16))
                if g >= 3:
                    pe.wait_ge(slots_copied, nth(b, GROUPS, g - 2))
                elif b + 1 < B:
                    if g == 0:
                        pe.wait_ge(r_copied, nth(b + 1, 4, 4))
                    else:
                        pe.wait_ge(x_added, nth(b + 1, 4, 2 + g))
                elif g == 0:
                    pe.wait_ge(turned_sb, nth(b, 6, 6))
                elif g == 1:
                    pe.wait_ge(rows_made, nth(b, 1, 1))
                else:
                    pe.wait_ge(logits_copied, nth(b, 2, 2))
                for j in range(4):
                    mm = nc.tensor.transpose(bank[g % 3][:, P * j:P * j + P], slot_x[:, 4 * g + j, :], ident[:, :])
                mm.then_inc(slots_turned, 1)

            def hidden_pair(b, e, j):
                c = e * HC + j
                cols = slice(e * SLOTS, e * SLOTS + COLS)
                if j == 0:
                    pe.wait_ge(slots_copied, nth(b, GROUPS, (e * SLOTS + COLS - 1) // (4 * P) + 1))
                    if not later(b):
                        pe.wait_ge(expert_weights_in[e], 48)
                if c >= 2 or later(b):
                    pe.wait_ge(prod_made, nth(b, POINTS, c - 1))
                nc.tensor.matmul(pair[c % 2][0][:, 0:COLS], gate_sb[:, e, P * j:P * j + P], slotT[:, cols],
                                 start=True, stop=True).then_inc(g_made, 1)
                nc.tensor.matmul(pair[c % 2][1][:, 0:COLS], fc_sb[:, e, P * j:P * j + P], slotT[:, cols],
                                 start=True, stop=True).then_inc(h_made, 1)

            def project(b, e):
                pe.wait_ge(hidden_made, nth(b, 2 * E, 2 * e + 2))
                if e or later(b):
                    pe.wait_ge(o_copied, nth(b, E, e))
                for i in range(PARTS):
                    for c in range(HC):
                        mm = nc.tensor.matmul(ps_o[0:PART, P * i:P * i + P],
                                              hidden[:, e % 2, c, PART * i:PART * i + PART], proj_sb[:, e, c, :],
                                              start=(c == 0), stop=(c == HC - 1))
                mm.then_inc(o_made, 1)

            def period(b):
                for point in range(POINTS):
                    e, j = divmod(point, HC)
                    if b >= 0:
                        hidden_pair(b, e, j)
                        if point < 2:
                            turn_slots(b, 3 + point)
                        if j == 2 and e > 0:
                            project(b, e - 1)
                    if b + 1 < B and b + 1 >= 0:
                        for name, n in TENSOR_ROUTE.get(point, ()):
                            stages[name](b + 1, n)
                    if b + 2 < B:
                        for name, n in TENSOR_MIX.get(point, ()):
                            stages[name](b + 2, n)
                if b >= 0:
                    project(b, E - 1)
                if 0 <= b + 1 < B:
                    for g in range(3):
                        turn_slots(b + 1, g)

            pe.wait_ge(consts_made, 6)
            pe.wait_ge(mix_weights_in, 16 * 4)
            for i in range(4 * L):
                mm = nc.tensor.transpose(bank[i // 4][:, P * (i % 4):P * (i % 4) + P], w_raw[:, i, :], ident[:, :])
            mm.then_inc(weights_turned, 1)
            pe.wait_ge(weights_copied, 2)
            pe.wait_ge(small_in, 16 * 6)
            for b in range(-2, B):
                period(b)

        @block.scalar
        def _(act):
            def turned(b, n):
                act.wait_ge(turned_ps, nth(b, 6, n + 1))
                half = n % 2
                if n >= 2 and n < 4:
                    act.wait_ge(r_made, nth(b, 4, n - 1))
                elif n >= 4:
                    act.wait_ge(r_made, nth(b, 4, n - 1))
                elif later(b):
                    act.wait_ge(logits_made, nth(b - 1, 2, half + 1))
                dst = normT[:, HALF * half:HALF * half + HALF]
                if n < 4:
                    nc.scalar.activation(dst, bank[0][:, :], ACT.Identity, bias=lnb_sb[:, n // 2:n // 2 + 1],
                                         scale=lnw_sb[:, n // 2:n // 2 + 1]).then_inc(turned_sb, 1)
                else:
                    nc.scalar.activation(dst, bank[0][:, :], ACT.Copy).then_inc(turned_sb, 1)

            def kr(b, n):
                half = slice(HALF * (n % 2), HALF * (n % 2) + HALF)
                act.wait_ge(k_made, nth(b, 4, n + 1))
                if n >= 2 or later(b):
                    act.wait_ge(kv_made, nth(b, 4, n - 1))
                nc.scalar.activation(k_sb[:, half], bank[1][:, :], ACT.Copy, scale=(1.0 - DECAY) / 2)\
                  .then_inc(k_copied, 1)
                act.wait_ge(r_made, nth(b, 4, n + 1))
                if n >= 2 or later(b):
                    act.wait_ge(mixed_made, nth(b, 4, n - 1))
                nc.scalar.activation(gate_r[:, half], bank[0][:, :], ACT.Tanh, scale=0.5).then_inc(r_copied, 1)

            def lead(b, _):
                act.wait_ge(gap_made, nth(b, 1, 1))
                if later(b):
                    act.wait_ge(share_made, nth(b - 1, 1, 1))
                nc.scalar.activation(gap_t[:, :], gap[:, :], ACT.Tanh, scale=0.5).then_inc(gap_turned, 1)

            stages = {"turned": turned, "kr": kr, "lead": lead}

            def copy_slots(b, g):
                act.wait_ge(slots_turned, nth(b, GROUPS, g + 1))
                if later(b):
                    act.wait_ge(h_made, nth(b - 1, POINTS, POINTS))
                nc.scalar.activation(slotT[:, 4 * P * g:4 * P * g + 4 * P], bank[g % 3][:, :], ACT.Copy)\
                  .then_inc(slots_copied, 1)

            def gate_copy(b, e, j):
                c = e * HC + j
                act.wait_ge(g_made, nth(b, POINTS, c + 1))
                if c >= 2 or later(b):
                    act.wait_ge(prod_made, nth(b, POINTS, c - 1))
                nc.scalar.activation(gate_s[:, c % 2, :], pair[c % 2][0][:, 0:COLS], ACT.Identity,
                                     bias=bgate_sb[:, e, j:j + 1]).then_inc(g_copied, 1)

            def silu(b, e, i):
                act.wait_ge(prod_made, nth(b, POINTS, e * HC + 2 * i + 2))
                if e >= 2 or later(b):
                    act.wait_ge(o_made, nth(b, E, e - 1))
                nc.scalar.activation(hidden[:, e % 2, 2 * i:2 * i + 2, 0:COLS], prod[:, e % 2, 2 * i:2 * i + 2, :],
                                     ACT.Silu).then_inc(hidden_made, 1)

            def period(b):
                for point in range(POINTS):
                    e, j = divmod(point, HC)
                    if b >= 0:
                        gate_copy(b, e, j)
                        if point < 2:
                            copy_slots(b, 3 + point)
                        if j == 1 and e > 0:
                            silu(b, e - 1, 1)
                        if j == 3:
                            silu(b, e, 0)
                    if b + 1 < B and b + 1 >= 0:
                        for name, n in SCALAR_ROUTE.get(point, ()):
                            stages[name](b + 1, n)
                    if b + 2 < B:
                        for name, n in SCALAR_MIX.get(point, ()):
                            stages[name](b + 2, n)
                if b >= 0:
                    silu(b, E - 1, 1)
                if 0 <= b + 1 < B:
                    for g in range(3):
                        copy_slots(b + 1, g)

            for i, w in enumerate((Wk, Wv, Wr, Wo)):
                act.dma_start(w_raw[:, L * i:L * i + L, :], w.rearrange("l e d -> e l d")).then_inc(mix_weights_in, 16)
            with nc.allow_non_contiguous_dma("per-feature columns"):
                act.dma_start(lnw_sb[:, :], ln_w.rearrange("l d -> d l")).then_inc(small_in, 16)
                act.dma_start(lnb_sb[:, :], ln_b.rearrange("l d -> d l")).then_inc(small_in, 16)
                act.dma_start(bfc_sb[:, :, :], b_fc.rearrange("e a (c p) -> p e (a c)", p=P)).then_inc(small_in, 16)
                act.dma_start(bgate_sb[:, :, :], b_gate.rearrange("e a (c p) -> p e (a c)", p=P)).then_inc(small_in, 16)
            act.dma_start(router_sb[:, :], router_w).then_inc(small_in, 16)
            act.dma_start(rbias_sb[:, :], router_b.partition_broadcast(P)).then_inc(small_in, 16)
            act.dma_start(bproj_sb[:, :, :], b_proj.rearrange("e a d -> (e a d)").partition_broadcast(P))\
               .then_inc(bproj_in, 16)
            act.wait_ge(small_in, 16 * 6)
            act.wait_ge(weights_turned, 1)
            for i in range(2):
                nc.scalar.activation(w_mix[:, 4 * i:4 * i + 4, :],
                                     bank[i][:, :].rearrange("p (w d) -> p w d", w=4), ACT.Copy)\
                  .then_inc(weights_copied, 1)
            for b in range(-2, B):
                period(b)

        @block.vector
        def _(dve):
            def stats_of(b, n):
                norm, half = divmod(n, 2)
                source = (x_in, x_mid, x_sum)[norm]
                if norm == 0 and half == 0:
                    dve.wait_ge(x_loaded, nth(b, 16, 16))
                if norm > 0:
                    dve.wait_ge(x_added, nth(b, 4, n - 1))
                if later(b):
                    dve.wait_ge(normed_made, nth(b - 1, 6, n + 1))
                for j in range(HT * half, HT * half + HT):
                    i = nc.vector.bn_stats(stats[:, norm, j, :], source[:, j, :])
                i.then_inc(stats_made, 1)
                dve.wait_ge(stats_made, nth(b, 6, n + 1))
                for j in range(HT * half, HT * half + HT):
                    i = nc.vector.bn_aggr(moments[:, norm, j, :], stats[:, norm, j, :])
                i.then_inc(moments_made, 1)

            def norm_of(b, n):
                norm, half = divmod(n, 2)
                source = (x_in, x_mid, x_sum)[norm]
                dve.wait_ge(rstd_made, nth(b, 6, n + 1))
                if norm == 0 and later(b):
                    dve.wait_ge(turned_ps, nth(b - 1, 6, 3 + half))
                elif norm == 1:
                    dve.wait_ge(turned_ps, nth(b, 6, 1 + half))
                elif norm == 2 and b >= RING:
                    dve.wait_ge(y_made, nth(b - RING, 2, 2))
                dve.wait_ge(moments_made, nth(b, 6, n + 1))
                dst = normed if norm < 2 else x_ln[:, b % RING, :, :]
                for j in range(HT * half, HT * half + HT):
                    i = nc.vector.tensor_scalar(dst[:, j, :], source[:, j, :], moments[:, norm, j, 0:1],
                                                rstd[:, norm, j:j + 1], ALU.subtract, ALU.mult)
                i.then_inc(normed_made, 1)

            def mix(b, n):
                lo, hi = HALF * (n % 2), HALF * (n % 2) + HALF
                dve.wait_ge(k_copied, nth(b, 4, n + 1))
                dve.wait_ge(v_made, nth(b, 4, n + 1))
                if n >= 2 or later(b):
                    dve.wait_ge(state_made, nth(b, 4, n - 1))
                nc.vector.tensor_tensor(kv_sb[:, lo:hi], bank[2][:, :], k_sb[:, lo:hi], ALU.mult).then_inc(kv_made, 1)
                dve.wait_ge(kv_made, nth(b, 4, n + 1))
                if n >= 2 or later(b):
                    dve.wait_ge(mixed_made, nth(b, 4, n - 1))
                if n % 2:
                    dve.wait_ge(state_made, nth(b, 4, n))
                nc.vector.tensor_tensor_scan(state[:, lo:hi], decay[:, :], kv_sb[:, lo:hi],
                                             state[:, lo - 1:lo] if n % 2 else 0.0, ALU.mult, ALU.add)\
                  .then_inc(state_made, 1)
                dve.wait_ge(r_copied, nth(b, 4, n + 1))
                dve.wait_ge(state_made, nth(b, 4, n + 1))
                if n >= 2 or later(b):
                    dve.wait_ge(out_made, nth(b, 4, n - 1))
                nc.vector.scalar_tensor_tensor(mixed[:, lo:hi], gate_r[:, lo:hi], 1.0, state[:, lo:hi],
                                               ALU.add, ALU.mult).then_inc(mixed_made, 1)

            def add(b, n):
                layer, half = divmod(n, 2)
                tiles = slice(HT * half, HT * half + HT)
                dve.wait_ge(out_made, nth(b, 4, n + 1))
                if layer == 0:
                    if later(b):
                        dve.wait_ge(skip_made, nth(b - 1, 1, 1))
                        dve.wait_ge(normed_made, nth(b - 1, 6, 3 + half))
                    src, dst = x_in, x_mid
                else:
                    dve.wait_ge(skip_made, nth(b, 1, 1))
                    if later(b):
                        dve.wait_ge(normed_made, nth(b - 1, 6, 5 + half))
                    src, dst = x_skip, x_sum
                nc.vector.tensor_tensor(dst[:, tiles, :], src[:, tiles, :],
                                        bank[1 + half][:, :].rearrange("p (j d) -> p j d", d=P), ALU.add)\
                  .then_inc(x_added, 1)

            def top(b, half):
                tiles = range(HT * half, HT * half + HT)
                dve.wait_ge(small_in, 16 * 6)
                dve.wait_ge(logits_made, nth(b, 2, half + 1))
                if later(b):
                    dve.wait_ge(top_index_made, nth(b - 1, 2, half + 1))
                nc.vector.tensor_tensor(logit[:, HT * half:HT * half + HT, :],
                                        bank[2][:, 0:HT * E].rearrange("p (j e) -> p j e", e=E),
                                        rbias_sb[:, :].rearrange("p (o e) -> p o e", o=1).to_broadcast([P, HT, E]),
                                        ALU.add).then_inc(logits_copied, 1)
                dve.wait_ge(logits_copied, nth(b, 2, half + 1))
                if later(b):
                    dve.wait_ge(gap_made, nth(b - 1, 1, 1))
                for j in tiles:
                    i = nc.vector.max(top_v[:, j, :], logit[:, j, :])
                i.then_inc(top_made, 1)
                dve.wait_ge(top_made, nth(b, 2, half + 1))
                if later(b):
                    dve.wait_ge(top_copied, nth(b - 1, 1, 1))
                for j in tiles:
                    i = nc.vector.max_index(top_i[:, j, :], top_v[:, j, :], logit[:, j, :])
                i.then_inc(top_index_made, 1)

            def choice(b, _):
                dve.wait_ge(top_made, nth(b, 2, 2))
                if later(b):
                    dve.wait_ge(gap_turned, nth(b - 1, 1, 1))
                nc.vector.tensor_tensor(gap[:, :], top_v[:, :, 0:1].rearrange("p j o -> p (j o)"),
                                        top_v[:, :, 1:2].rearrange("p j o -> p (j o)"), ALU.subtract)\
                  .then_inc(gap_made, 1)
                dve.wait_ge(top_index_made, nth(b, 2, 2))
                if later(b):
                    dve.wait_ge(chosen_made, nth(b - 1, 1, 1))
                nc.vector.tensor_copy(top_f[:, :, :], top_i[:, :, 0:K]).then_inc(top_copied, 1)
                dve.wait_ge(top_copied, nth(b, 1, 1))
                dve.wait_ge(consts_made, 6)
                if later(b):
                    dve.wait_ge(rows_made, nth(b - 1, 1, 1))
                nc.vector.tensor_tensor(
                    chosen[:, :, :, :].rearrange("p j k e -> p (j k) e"),
                    expert_id[:, :].rearrange("p (c e) -> p c e", e=E),
                    top_f[:, :, :].rearrange("p j (k o) -> p (j k) o", o=1).to_broadcast([P, TILES * K, E]),
                    ALU.is_equal).then_inc(chosen_made, 1)

            def rows(b, _):
                counts = bank[1][:, 0:TILES * K * E]
                picks = chosen[:, :, :, :].rearrange("p j k e -> p (j k) e")
                dve.wait_ge(counts_made, nth(b, 1, 1))
                dve.wait_ge(chosen_made, nth(b, 1, 1))
                nc.vector.scalar_tensor_tensor(row_in[:, :], counts, float(CAP), expert_base[:, :],
                                               ALU.min, ALU.add).then_inc(rows_step, 1)
                nc.vector.tensor_scalar(row_far[:, :], counts, float(CAP), FAR, ALU.is_gt, ALU.mult)\
                  .then_inc(rows_step, 1)
                dve.wait_ge(rows_step, nth(b, 5, 2))
                nc.vector.tensor_tensor(row_both[:, 0, :, :], row_in[:, :].rearrange("p (c e) -> p c e", e=E),
                                        picks, ALU.mult).then_inc(rows_step, 1)
                nc.vector.tensor_tensor(row_far[:, :], row_far[:, :], row_in[:, :], ALU.add).then_inc(rows_step, 1)
                dve.wait_ge(rows_step, nth(b, 5, 4))
                nc.vector.tensor_tensor(row_both[:, 1, :, :], row_far[:, :].rearrange("p (c e) -> p c e", e=E),
                                        picks, ALU.mult).then_inc(rows_step, 1)
                dve.wait_ge(rows_step, nth(b, 5, 5))
                nc.vector.tensor_reduce(row_f[:, :, :].rearrange("p w c -> p (w c)"),
                                        row_both[:, :, :, :].rearrange("p w c e -> p (w c) e"), AX.X, ALU.add)\
                  .then_inc(rows_reduced, 1)
                dve.wait_ge(rows_reduced, nth(b, 1, 1))
                if b >= RING:
                    for i in range(2):
                        dve.wait_ge(gathered[i], nth(b - RING, 16 * TILES, 16 * TILES))
                if later(b):
                    dve.wait_ge(scattered, nth(b - 1, 16 * TILES * K, 16 * TILES * K))
                nc.vector.tensor_copy(row_from[:, b % RING, :], row_f[:, 0, :])
                nc.vector.tensor_copy(row_to[:, :], row_f[:, 1, :]).then_inc(rows_made, 1)

            stages = {"stats": stats_of, "norm": norm_of, "mix": mix, "add": add, "top": top,
                      "choice": choice, "rows": rows}

            def gather_sum(b, half):
                dve.wait_ge(gathered[half], nth(b, 16 * TILES, 16 * TILES))
                dve.wait_ge(share_made, nth(b, 1, 1))
                if later(b):
                    dve.wait_ge(y_made, nth(b - 1, 2, 2))
                for j in range(HT * half, HT * half + HT):
                    i = nc.vector.scalar_tensor_tensor(part_sum[:, j, :], picked[:, j, 0, :], share[:, b % RING, j, 0:1],
                                                       x_ln[:, b % RING, j, :], ALU.mult, ALU.add)
                i.then_inc(part_made, 1)
                dve.wait_ge(part_made, nth(b, 2, half + 1))
                if later(b):
                    dve.wait_ge(y_normed, nth(b - 1, 2, 2))
                for j in range(HT * half, HT * half + HT):
                    i = nc.vector.scalar_tensor_tensor(y_sum[:, j, :], picked[:, j, 1, :], share[:, b % RING, j, 1:2],
                                                       part_sum[:, j, :], ALU.mult, ALU.add)
                i.then_inc(y_made, 1)
                dve.wait_ge(y_made, nth(b, 2, half + 1))
                for j in range(HT * half, HT * half + HT):
                    i = nc.vector.bn_stats(y_stats[:, j, :], y_sum[:, j, :])
                i.then_inc(y_stats_made, 1)
                dve.wait_ge(y_stats_made, nth(b, 2, half + 1))
                for j in range(HT * half, HT * half + HT):
                    i = nc.vector.bn_aggr(y_moments[:, j, :], y_stats[:, j, :])
                i.then_inc(y_moments_made, 1)

            def final_norm(b, half):
                dve.wait_ge(y_rstd_made, nth(b, 2, half + 1))
                dve.wait_ge(y_moments_made, nth(b, 2, half + 1))
                if later(b):
                    dve.wait_ge(out_stored, nth(b - 1, 32, 32))
                for j in range(HT * half, HT * half + HT):
                    i = nc.vector.tensor_scalar(y_out[:, j, :], y_sum[:, j, :], y_moments[:, j, 0:1],
                                                y_rstd[:, j:j + 1], ALU.subtract, ALU.mult)
                i.then_inc(y_normed, 1)

            combine_stages = {"gather_sum": gather_sum, "final_norm": final_norm}

            def product(b, e, j):
                c = e * HC + j
                dve.wait_ge(h_made, nth(b, POINTS, c + 1))
                dve.wait_ge(g_copied, nth(b, POINTS, c + 1))
                if j == 0 and (e >= 2 or later(b)):
                    dve.wait_ge(hidden_made, nth(b, 2 * E, 2 * e - 2))
                nc.vector.scalar_tensor_tensor(prod[:, e % 2, j, :], pair[c % 2][1][:, 0:COLS], bfc_sb[:, e, j:j + 1],
                                               gate_s[:, c % 2, :], ALU.add, ALU.mult).then_inc(prod_made, 1)

            def copy_out(b, e):
                dve.wait_ge(o_made, nth(b, E, e + 1))
                dve.wait_ge(bproj_in, 16)
                if later(b):
                    dve.wait_ge(o_stored, nth(b - 1, 16 * E, 16 * E))
                nc.vector.tensor_tensor(o_sb[:, e, :, :],
                                        ps_o[0:PART, 0:PARTS * P].rearrange("p (i d) -> p i d", d=P),
                                        bproj_sb[0:PART, e:e + 1, :].to_broadcast([PART, PARTS, P]), ALU.add)\
                  .then_inc(o_copied, 1)

            def period(b):
                for point in range(POINTS):
                    e, j = divmod(point, HC)
                    if 0 <= b < B:
                        product(b, e, j)
                        if j == 3 and e > 0:
                            copy_out(b, e - 1)
                    if b > 0:
                        for name, n in VECTOR_COMBINE.get(point, ()):
                            combine_stages[name](b - 1, n)
                    if b + 1 < B and b + 1 >= 0:
                        for name, n in VECTOR_ROUTE.get(point, ()):
                            stages[name](b + 1, n)
                    if b + 2 < B:
                        for name, n in VECTOR_MIX.get(point, ()):
                            stages[name](b + 2, n)
                if 0 <= b < B:
                    copy_out(b, E - 1)

            nc.vector.memset(decay[:, :], DECAY).then_inc(vector_consts, 1)
            nc.vector.memset(hidden[:, :, :, :], 0.0).then_inc(vector_consts, 1)
            dve.wait_ge(vector_consts, 2)
            for b in range(-2, B + 1):
                period(b)

        @block.gpsimd
        def _(pool):
            def rstd_of(b, n):
                norm, half = divmod(n, 2)
                tiles = slice(HT * half, HT * half + HT)
                pool.wait_ge(moments_made, nth(b, 6, n + 1))
                if later(b):
                    pool.wait_ge(normed_made, nth(b - 1, 6, n + 1))
                nc.gpsimd.tensor_scalar(shifted[:, norm, tiles],
                                        moments[:, norm, tiles, 1:2].rearrange("p j o -> p (j o)"),
                                        EPS, None, ALU.add).then_inc(shifted_made, 1)
                pool.wait_ge(shifted_made, nth(b, 6, n + 1))
                nc.gpsimd.tensor_tensor(rstd[:, norm, tiles], shifted[:, norm, tiles], power[:, :], ALU.pow)\
                  .then_inc(rstd_made, 1)

            def skip_sum(b, _):
                pool.wait_ge(x_added, nth(b, 4, 2))
                pool.wait_ge(x_loaded, nth(b, 16, 16))
                if later(b):
                    pool.wait_ge(x_added, nth(b - 1, 4, 4))
                nc.gpsimd.tensor_tensor(x_skip[:, :, :], x_in[:, :, :], x_mid[:, :, :], ALU.add)\
                  .then_inc(skip_made, 1)

            def shares(b, _):
                pool.wait_ge(gap_turned, nth(b, 1, 1))
                if b >= RING:
                    pool.wait_ge(y_made, nth(b - RING, 2, 2))
                nc.gpsimd.tensor_scalar(share[:, b % RING, :, 0:1].rearrange("p j o -> p (j o)"), gap_t[:, :], 0.5, 0.5,
                                        ALU.mult, ALU.add)
                nc.gpsimd.tensor_scalar(share[:, b % RING, :, 1:2].rearrange("p j o -> p (j o)"), gap_t[:, :], -0.5, 0.5,
                                        ALU.mult, ALU.add).then_inc(share_made, 1)

            def scatter(b, j):
                if j == 0:
                    pool.wait_ge(rows_made, nth(b, 1, 1))
                    pool.wait_ge(normed_made, nth(b, 6, 6))
                    if later(b):
                        for g in range(GROUPS):
                            pool.wait_ge(slots_loaded[g], nth(b - 1, 16, 16))
                    else:
                        pool.wait_ge(rows_zeroed, 16 * GROUPS)
                for k in range(K):
                    c = j * K + k
                    nc.gpsimd.indirect_dma_start(
                        out=slot_rows, out_offset=bass.IndirectOffsetOnAxis(ap=row_to[:, c:c + 1], axis=0),
                        in_=x_ln[:, b % RING, j, :], in_offset=None, bounds_check=ROWS - 1, oob_is_err=False)\
                      .then_inc(scattered, 16)

            stages = {"rstd": rstd_of, "skip_sum": skip_sum, "shares": shares, "scatter": scatter}

            def gather(b, j):
                half = j // HT
                if j == 0:
                    pool.wait_ge(o_stored, nth(b, 16 * E, 16 * E))
                if j % HT == 0 and later(b):
                    pool.wait_ge(y_made, nth(b - 1, 2, half + 1))
                for k in range(K):
                    c = j * K + k
                    nc.gpsimd.indirect_dma_start(
                        out=picked[:, j, k, :], out_offset=None, in_=expert_rows,
                        in_offset=bass.IndirectOffsetOnAxis(ap=row_from[:, b % RING, c:c + 1], axis=0),
                        bounds_check=E * SLOTS - 1, oob_is_err=False).then_inc(gathered[half], 16)

            def final_rstd(b, half):
                tiles = slice(HT * half, HT * half + HT)
                pool.wait_ge(y_moments_made, nth(b, 2, half + 1))
                if later(b):
                    pool.wait_ge(y_normed, nth(b - 1, 2, 2))
                nc.gpsimd.tensor_scalar(y_shifted[:, tiles],
                                        y_moments[:, tiles, 1:2].rearrange("p j o -> p (j o)"),
                                        EPS, None, ALU.add).then_inc(y_shifted_made, 1)
                pool.wait_ge(y_shifted_made, nth(b, 2, half + 1))
                nc.gpsimd.tensor_tensor(y_rstd[:, tiles], y_shifted[:, tiles], power[:, :], ALU.pow)\
                  .then_inc(y_rstd_made, 1)

            combine_stages = {"gather": gather, "final_rstd": final_rstd}

            def period(b):
                for point in range(POINTS):
                    if b > 0:
                        for name, n in POOL_COMBINE.get(point, ()):
                            combine_stages[name](b - 1, n)
                    if b + 1 < B and b + 1 >= 0:
                        for name, n in POOL_ROUTE.get(point, ()):
                            stages[name](b + 1, n)
                    if b + 2 < B:
                        for name, n in POOL_MIX.get(point, ()):
                            stages[name](b + 2, n)

            nc.gpsimd.memset(slot_x[:, :, :], 0.0).then_inc(zeroed, 1)
            nc.gpsimd.memset(ident[:, :], 0.0).then_inc(pool_consts, 1)
            nc.gpsimd.memset(ones[:, :], 1.0).then_inc(consts_made, 1)
            nc.gpsimd.memset(power[:, :], -0.5).then_inc(consts_made, 1)
            nc.gpsimd.memset(upto[:, :], 1.0).then_inc(pool_consts, 1)
            pool.wait_ge(pool_consts, 2)
            nc.gpsimd.affine_select(out=ident[:, :], in_=ident[:, :], compare_op=ALU.not_equal, fill=1.0, base=0,
                                    pattern=[[-1, P]], channel_multiplier=1).then_inc(consts_made, 1)
            nc.gpsimd.affine_select(out=upto[:, :], in_=upto[:, :], compare_op=ALU.is_ge, fill=0.0, base=0,
                                    pattern=[[1, P]], channel_multiplier=-1).then_inc(consts_made, 1)
            nc.gpsimd.iota(expert_id[:, :], pattern=[[0, TILES * K], [1, E]], base=0, channel_multiplier=0,
                           allow_small_or_imprecise_dtypes=True).then_inc(consts_made, 1)
            nc.gpsimd.iota(expert_base[:, :], pattern=[[0, TILES * K], [SLOTS, E]], base=-1, channel_multiplier=0,
                           allow_small_or_imprecise_dtypes=True).then_inc(consts_made, 1)
            pool.wait_ge(consts_made, 6)
            for b in range(-2, B + 1):
                period(b)


_INPUTS = ["L0_attn_h", "L0_attn_ln_w", "L0_attn_ln_b", "L0_attn_Wk", "L0_attn_Wv", "L0_attn_Wr", "L0_attn_Wo",
           "L0_ffn_router_w", "L0_ffn_router_b", "L0_ffn_w_c_fc", "L0_ffn_b_c_fc", "L0_ffn_w_gate",
           "L0_ffn_b_gate", "L0_ffn_w_c_proj", "L0_ffn_b_c_proj"]


def kernel(**inputs):
    import concourse.bacc as bacc
    from concourse.bass_utils import run_bass_kernel_spmd

    nc = bacc.Bacc("TRN2", target_bir_lowering=False, num_devices=1)
    arrays, args = {}, []
    for name in _INPUTS:
        a = np.ascontiguousarray(inputs[name])
        arrays[f"in_{name}"] = a
        args.append(nc.dram_tensor(f"in_{name}", a.shape, mybir.dt.from_np(a.dtype), kind="ExternalInput").ap())
    args.append(nc.dram_tensor("out_0", (B, T, P), F32, kind="ExternalOutput").ap())
    time_mix_moe(nc, *args)
    r = run_bass_kernel_spmd(nc, [arrays], core_ids=[0])
    return r.results[0]["out_0"]
```

```python
from contextlib import ExitStack

import numpy as np
import concourse.bass as bass
from concourse import mybir

ALU = mybir.AluOpType
ACT = mybir.ActivationFunctionType
AX = mybir.AxisListType
F32 = mybir.dt.float32
F32R = mybir.dt.float32r
BF16 = mybir.dt.bfloat16
U32 = mybir.dt.uint32

P = 128
B, T, L = 4, 1024, 2
TILES = T // P
HT = TILES // 2
HALF = HT * P
QUARTERS = 4
QT = TILES // QUARTERS
E, K, H = 8, 2, 512
HC = H // P
CAP = int(1.2 * K * T // E)
COLS = CAP + CAP % 2
PART = 104
PARTS = 3
SLOTS = PART * PARTS
GROUPS = -(-E * SLOTS // (4 * P))
ROWS = GROUPS * 4 * P
POINTS = E * HC
FAR = float(1 << 20)
EPS = 1e-5
DECAY = 0.95

assert CAP <= COLS <= SLOTS and L == 2 and K == 2

RING = 3
OUT_RING = 3
SLOT_RING = 3

TENSOR_HEAD = [("turn", 0, 0), ("kvr", 0, 0), ("turn", 0, 1), ("kvr", 0, 1), ("out", 0, 0), ("out", 0, 1),
               ("turn", 0, 2), ("kvr", 0, 2), ("turn", 0, 3), ("kvr", 0, 3), ("turn", 1, 0), ("out", 0, 2),
               ("out", 0, 3), ("kvr", 1, 0), ("turn", 0, 4), ("turn", 1, 1), ("turn", 0, 5), ("logits", 0, 0),
               ("logits", 0, 1), ("out", 1, 0), ("count", 0, 0), ("kvr", 1, 1), ("out", 1, 1), ("turn", 1, 2),
               ("kvr", 1, 2), ("turn", 1, 3), ("kvr", 1, 3), ("out", 1, 2), ("out", 1, 3)]
SCALAR_HEAD = [("turned", 0, 0), ("high", 0, 0), ("kr", 0, 0), ("turned", 0, 1), ("high", 1, 0), ("kr", 0, 1),
               ("turned", 0, 2), ("high", 2, 0), ("kr", 0, 2), ("turned", 0, 3), ("high", 3, 0), ("kr", 0, 3),
               ("turned", 1, 0), ("high", 4, 0), ("high", 5, 0), ("kr", 1, 0), ("turned", 0, 4), ("turned", 1, 1),
               ("high", 6, 0), ("turned", 0, 5), ("high", 7, 0), ("lead", 0, 0), ("kr", 1, 1), ("turned", 1, 2),
               ("kr", 1, 2), ("turned", 1, 3), ("kr", 1, 3)]
VECTOR_HEAD = [("stats", 0, 0), ("stats", 0, 1), ("norm", 0, 0), ("norm", 0, 1), ("mix", 0, 0), ("mix", 0, 1),
               ("add", 0, 0), ("stats", 0, 2), ("add", 0, 1), ("stats", 0, 3), ("norm", 0, 2), ("norm", 0, 3),
               ("skip_sum", 0, 0), ("stats", 1, 0), ("mix", 0, 2), ("norm", 1, 0), ("mix", 0, 3), ("add", 0, 2),
               ("stats", 0, 4), ("add", 0, 3), ("stats", 1, 1), ("norm", 0, 4), ("stats", 0, 5), ("norm", 1, 1),
               ("norm", 0, 5), ("mix", 1, 0), ("top", 0, 0), ("top", 0, 1), ("choice", 0, 0), ("add", 1, 0),
               ("rows", 0, 0), ("stats", 1, 2), ("mix", 1, 1), ("norm", 1, 2), ("add", 1, 1), ("stats", 1, 3),
               ("norm", 1, 3), ("skip_sum", 1, 0), ("mix", 1, 2), ("mix", 1, 3), ("add", 1, 2), ("stats", 1, 4),
               ("add", 1, 3), ("stats", 2, 0), ("stats", 1, 5), ("stats", 2, 1)]
POOL_HEAD = [("rstd", 0, 0), ("rstd", 0, 1), ("low", 0, 0), ("low", 1, 0), ("rstd", 0, 2), ("rstd", 0, 3),
             ("low", 2, 0), ("rstd", 1, 0), ("low", 3, 0), ("low", 4, 0), ("rstd", 0, 4), ("rstd", 1, 1),
             ("rstd", 0, 5), ("low", 5, 0), ("low", 6, 0), ("low", 7, 0), ("shares", 0, 0), ("scatter", 0, 0),
             ("scatter", 0, 1), ("rstd", 1, 2), ("scatter", 0, 2), ("scatter", 0, 3), ("rstd", 1, 3),
             ("scatter", 0, 4), ("scatter", 0, 5), ("scatter", 0, 6), ("scatter", 0, 7), ("rstd", 1, 4),
             ("rstd", 1, 5), ("rstd", 2, 0), ("rstd", 2, 1)]

FILL = {("weights", 0, 0): 12, ("turn", 0, 0): 5, ("kvr", 0, 0): 5, ("kvr", 0, 1): 1, ("turn", 0, 2): 11,
        ("kvr", 0, 2): 4, ("kvr", 0, 3): 1, ("turn", 0, 4): 3, ("turn", 0, 5): 6, ("turn", 1, 2): 9, ("kvr", 1, 2): 2,
        ("kvr", 1, 3): 2, ("slots", 0, 0): 10}

TENSOR_MIX = {9: [("turn", 0)], 10: [("kvr", 0)], 12: [("turn", 1)], 13: [("kvr", 1)], 14: [("out", 0)],
              17: [("out", 1)], 18: [("turn", 2)], 20: [("kvr", 2)], 21: [("turn", 3)], 22: [("kvr", 3)],
              24: [("out", 2)], 26: [("out", 3)]}
TENSOR_ROUTE = {2: [("turn", 4)], 3: [("turn", 5)], 4: [("logits", 0)], 5: [("logits", 1)], 8: [("count", 0)]}
SCALAR_MIX = {9: [("turned", 0)], 10: [("kr", 0)], 12: [("turned", 1)], 13: [("kr", 1)], 19: [("turned", 2)],
              20: [("kr", 2)], 21: [("turned", 3)], 23: [("kr", 3)]}
SCALAR_ROUTE = {2: [("turned", 4)], 4: [("turned", 5)], 6: [("lead", 0)]}
VECTOR_MIX = {6: [("norm", 0)], 9: [("norm", 1)], 11: [("mix", 0)], 14: [("mix", 1)], 15: [("add", 0), ("stats", 2)],
              16: [("norm", 2)], 17: [("add", 1)], 18: [("stats", 3)], 19: [("norm", 3)], 20: [("skip_sum", 0)],
              21: [("mix", 2)], 23: [("mix", 3)], 24: [("add", 2)], 25: [("stats", 4)], 27: [("add", 3)],
              28: [("stats", 5)]}
VECTOR_AHEAD = {27: [("stats", 0)], 31: [("stats", 1)]}
VECTOR_ROUTE = {0: [("norm", 4)], 1: [("norm", 5)], 4: [("top", 0)], 5: [("top", 1), ("choice", 0)], 8: [("rows", 0)]}
VECTOR_COMBINE = {7: [("gather_sum", 0)], 9: [("gather_sum", 1)], 12: [("final_norm", 0)], 13: [("gather_sum", 2)],
                  16: [("final_norm", 1)], 19: [("final_norm", 2)], 22: [("gather_sum", 3)], 25: [("final_norm", 3)]}
VECTOR_COMBINE_LATE = {9: [("gather_sum", 0)], 12: [("gather_sum", 1)], 13: [("final_norm", 0)],
                       16: [("gather_sum", 2)], 17: [("final_norm", 1)], 20: [("gather_sum", 3)],
                       21: [("final_norm", 2)], 28: [("final_norm", 3)]}
POOL_MIX = {15: [("rstd", 2)], 17: [("rstd", 3)], 26: [("rstd", 4)], 31: [("rstd", 5)]}
POOL_AHEAD = {28: [("rstd", 0)], 31: [("rstd", 1)]}
POOL_ROUTE = {6: [("shares", 0)], 10: [("scatter", 0)], 12: [("scatter", 1)], 13: [("scatter", 2)],
              14: [("scatter", 3)], 15: [("scatter", 4)], 16: [("scatter", 5)], 18: [("scatter", 6)],
              20: [("scatter", 7)]}
POOL_COMBINE = {3: [("gather", 0)], 4: [("gather", 1)], 5: [("gather", 2)], 6: [("gather", 3)], 7: [("gather", 4)],
                8: [("gather", 5)], 9: [("gather", 6), ("final_rstd", 0)], 10: [("gather", 7)],
                13: [("final_rstd", 1)], 14: [("final_rstd", 2)], 23: [("final_rstd", 3)]}
PROJECTIONS = ({1: (0,), 2: (1,), 3: (2,)}, {2: (0,), 3: (1, 2)})
SLOT_TURNS = {6: (0, 3), 18: (0, 4), 28: (1, 0), 29: (1, 1), 30: (1, 2)}

VECTOR_TAIL = [("gather_sum", 0), ("gather_sum", 1), ("gather_sum", 2), ("final_norm", 0), ("gather_sum", 3),
               ("final_norm", 1), ("final_norm", 2), ("final_norm", 3)]
POOL_TAIL = [("gather", 0), ("gather", 1), ("gather", 2), ("gather", 3), ("gather", 4), ("gather", 5), ("gather", 6),
             ("gather", 7), ("final_rstd", 0), ("final_rstd", 1), ("final_rstd", 2), ("final_rstd", 3)]


def nth(b, per, k):
    return b * per + k


def step(b, n):
    return nth(b, 4, n + 1) if n < 4 else nth(b, 2, n - 3)


def mixed_by(b):
    return 4 * (max(b, 1) + 1)


def banks_between(b):
    return 2 if b < 2 else 1


def stored(b, i):
    return len([c for c in range(E * (b + 1)) if c % OUT_RING == i])


def later(b):
    return b > 0


def time_mix_moe(nc, h, ln_w, ln_b, Wk, Wv, Wr, Wo, router_w, router_b, w_fc, b_fc, w_gate, b_gate,
                 w_proj, b_proj, out):
    with ExitStack() as ctx:
        def sb(name, shape, dt=F32):
            return ctx.enter_context(nc.sbuf_tensor(name, shape, dt))

        def sem(name):
            return ctx.enter_context(nc.semaphore(name))

        ident = sb("ident", [P, P])
        upto = sb("upto", [P, P], BF16)
        ones = sb("ones", [P, P], BF16)
        decay = sb("decay", [P, HALF])
        power = sb("power", [P, HT])
        expert_id = sb("expert_id", [P, TILES * K * E])
        expert_base = sb("expert_base", [P, TILES * K * E])
        lnw_sb = sb("lnw_sb", [P, L])
        lnb_sb = sb("lnb_sb", [P, L])
        w_mix = sb("w_mix", [P, 4 * L, P])
        router_sb = sb("router_sb", [P, E])
        rbias_sb = sb("rbias_sb", [P, E])
        fc_hi = sb("fc_hi", [P, E, H], F32R)
        fc_lo = sb("fc_lo", [P, E, H], F32R)
        gate_hi = sb("gate_hi", [P, E, H], F32R)
        gate_lo = sb("gate_lo", [P, E, H], F32R)
        proj_sb = sb("proj_sb", [P, E, HC, P])
        bfc_sb = sb("bfc_sb", [P, E, HC])
        bgate_sb = sb("bgate_sb", [P, E, HC])
        bproj_sb = sb("bproj_sb", [P, E, P])
        x_in = sb("x_in", [P, 2, TILES, P])
        x_mid = sb("x_mid", [P, 2, TILES, P])
        normed = sb("normed", [P, TILES, P])
        stats = sb("stats", [P, 2, 3, TILES, 6])
        moments = sb("moments", [P, 2, 3, TILES, 2])
        shifted = sb("shifted", [P, 2, 3, TILES])
        rstd = sb("rstd", [P, 2, 3, TILES])
        normT = sb("normT", [P, T])
        kv_sb = sb("kv_sb", [P, T])
        state = sb("state", [P, T])
        mixed = sb("mixed", [P, T])
        x_ln = sb("x_ln", [P, RING, TILES, P])
        logit = sb("logit", [P, TILES, E])
        top_v = sb("top_v", [P, TILES, 8])
        top_i = sb("top_i", [P, TILES, 8], U32)
        top_f = sb("top_f", [P, TILES, K])
        gap = sb("gap", [P, TILES])
        gap_t = sb("gap_t", [P, TILES])
        share = sb("share", [P, RING, TILES, K])
        chosen = sb("chosen", [P, TILES, K, E], BF16)
        row_in = sb("row_in", [P, TILES * K * E])
        row_far = sb("row_far", [P, TILES * K * E])
        row_both = sb("row_both", [P, 2, TILES * K, E])
        row_f = sb("row_f", [P, 2, TILES * K])
        row_to = sb("row_to", [P, TILES * K], U32)
        row_from = sb("row_from", [P, RING, TILES * K], U32)
        slot_x = sb("slot_x", [P, SLOT_RING, 4, P])
        slotT_hi = sb("slotT_hi", [P, ROWS], F32R)
        slotT_lo = sb("slotT_lo", [P, ROWS], F32R)
        gate_s = sb("gate_s", [P, 2, COLS])
        prod = sb("prod", [P, 2, HC, COLS])
        hidden = sb("hidden", [P, 2, HC, SLOTS])
        o_sb = sb("o_sb", [PART, OUT_RING, PARTS, P])
        picked = sb("picked", [P, TILES, K, P])
        w_raw = picked[:, 0:L * 2, :, :].rearrange("p (w l) k d -> p (w l k) d", l=L)
        w_in = prod[:, :, :, :].rearrange("p r c s -> p r (c s)")[:, :, 0:2 * H]
        y_stats = sb("y_stats", [P, TILES, 6])
        y_moments = sb("y_moments", [P, TILES, 2])
        y_shifted = sb("y_shifted", [P, TILES])
        y_rstd = sb("y_rstd", [P, TILES])

        pair = [[ctx.enter_context(nc.psum_tensor(f"pair{i}{n}", [P, 512], F32)) for n in "gh"] for i in range(2)]
        ps_o = ctx.enter_context(nc.psum_tensor("ps_o", [P, 512], F32))
        bank = [ctx.enter_context(nc.psum_tensor(f"bank{i}", [P, 512], F32)) for i in range(3)]

        def mix_banks(b, n):
            if banks_between(b) == 2 and n % 2:
                return pair[0][0], pair[0][1], pair[1][0]
            return bank

        def out_bank(b, n):
            if b >= 2:
                return bank[1 + n % 2]
            return pair[1][1] if b == 0 and n % 2 else ps_o

        def route_banks(b):
            return (pair[1][1],) * 3 if b == 0 else bank

        def route_turned(b):
            return picked[:, HT:TILES, :, :].rearrange("p j k d -> p (j k d)") if b == 0 else normT

        slot_rows = nc.dram_tensor("slot_rows", [ROWS, P], F32, kind="Internal").ap()
        expert_rows = nc.dram_tensor("expert_rows", [E * SLOTS, P], F32, kind="Internal").ap()

        consts_made = sem("consts_made")
        mix_weights_in = sem("mix_weights_in")
        ln_in = sem("ln_in")
        router_in = sem("router_in")
        small_in = sem("small_in")
        expert_weights_in = [sem(f"expert_weights_in{i}") for i in range(2)]
        proj_in = sem("proj_in")
        bproj_in = sem("bproj_in")
        x_loaded = [sem(f"x_loaded{i}") for i in range(2)]
        weights_turned = sem("weights_turned")
        weights_copied = sem("weights_copied")
        stats_made = [sem("stats_made"), sem("stats_made_last")]
        moments_made = [sem("moments_made"), sem("moments_made_last")]
        shifted_made = [sem("shifted_made"), sem("shifted_made_last")]
        rstd_made = [sem("rstd_made"), sem("rstd_made_last")]
        normed_made = [sem("normed_made"), sem("normed_made_last")]
        turned_ps = [sem("turned_ps"), sem("turned_ps_last")]
        turned_sb = [sem("turned_sb"), sem("turned_sb_last")]
        k_made = sem("k_made")
        v_made = sem("v_made")
        r_made = sem("r_made")
        k_copied = sem("k_copied")
        r_copied = sem("r_copied")
        kv_made = sem("kv_made")
        state_made = sem("state_made")
        mixed_made = sem("mixed_made")
        out_made = sem("out_made")
        x_added = sem("x_added")
        skip_made = sem("skip_made")
        logits_made = sem("logits_made")
        logits_copied = sem("logits_copied")
        top_made = sem("top_made")
        top_index_made = sem("top_index_made")
        top_copied = sem("top_copied")
        chosen_made = sem("chosen_made")
        gap_made = sem("gap_made")
        gap_turned = sem("gap_turned")
        counts_made = sem("counts_made")
        rows_step = sem("rows_step")
        rows_made = sem("rows_made")
        rows_reduced = sem("rows_reduced")
        vector_consts = sem("vector_consts")
        pool_consts = sem("pool_consts")
        share_made = sem("share_made")
        zeroed = sem("zeroed")
        rows_zeroed = sem("rows_zeroed")
        scattered = sem("scattered")
        slots_loaded = [sem(f"slots_loaded{g}") for g in range(GROUPS)]
        slots_turned = sem("slots_turned")
        slots_high = sem("slots_high")
        slots_copied = sem("slots_copied")
        weights_high = sem("weights_high")
        weights_split = sem("weights_split")
        g_made = sem("g_made")
        h_made = sem("h_made")
        g_copied = sem("g_copied")
        prod_made = sem("prod_made")
        hidden_made = sem("hidden_made")
        o_made = sem("o_made")
        o_copied = sem("o_copied")
        o_stored = [sem(f"o_stored{i}") for i in range(OUT_RING)]
        gathered = [sem(f"gathered{q}") for q in range(QUARTERS)]
        part_made = sem("part_made")
        y_made = sem("y_made")
        y_stats_made = sem("y_stats_made")
        y_moments_made = sem("y_moments_made")
        y_shifted_made = sem("y_shifted_made")
        y_rstd_made = sem("y_rstd_made")
        y_normed = sem("y_normed")
        out_stored = sem("out_stored")

        h_view = h.rearrange("b (j p) d -> b p j d", p=P)
        out_view = out.rearrange("b (j p) d -> b p j d", p=P)
        slot_view = slot_rows.rearrange("(g j p) d -> g p j d", p=P, j=4)
        expert_view = expert_rows.rearrange("(e i p) d -> e p i d", i=PARTS, p=PART)

        block = ctx.enter_context(nc.Block())

        @block.sync
        def _(sp):
            def load_x(b):
                if b >= 2:
                    sp.wait_ge(normed_made[1], nth(b - 2, 2, 2))
                sp.dma_start(x_in[:, b % 2, :, :], h_view[b]).then_inc(x_loaded[b % 2], 16)

            def load_expert(e):
                if e >= 2:
                    sp.wait_ge(weights_split, e - 1)
                sp.dma_start(w_in[:, e % 2, 0:H], w_gate[e]).then_inc(expert_weights_in[e % 2], 16)
                sp.dma_start(w_in[:, e % 2, H:2 * H], w_fc[e]).then_inc(expert_weights_in[e % 2], 16)

            def load_slots(b, groups):
                for g in groups:
                    if g == 0:
                        sp.wait_ge(scattered, nth(b, 16 * TILES * K, 16 * TILES * K))
                        if later(b):
                            sp.wait_ge(slots_turned, nth(b - 1, GROUPS, GROUPS))
                        else:
                            sp.wait_ge(rows_zeroed, 16 * GROUPS)
                    elif g >= SLOT_RING:
                        sp.wait_ge(slots_turned, nth(b, GROUPS, g - SLOT_RING + 1))
                    sp.dma_start(slot_x[:, g % SLOT_RING, :, :], slot_view[g]).then_inc(slots_loaded[g], 16)

            def store_expert(b, e):
                if e == 0 and later(b):
                    for q in range(QUARTERS):
                        sp.wait_ge(gathered[q], nth(b - 1, 16 * K * QT, 16 * K * QT))
                sp.wait_ge(o_copied, nth(b, E, e + 1))
                i = (b * E + e) % OUT_RING
                sp.dma_start(expert_view[e], o_sb[:, i, :, :]).then_inc(o_stored[i], 16)

            def store_out(b):
                for q in range(QUARTERS):
                    sp.wait_ge(y_normed, nth(b, QUARTERS, q + 1))
                    sp.dma_start(out_view[b][:, QT * q:QT * q + QT, :],
                                 picked[:, QT * q:QT * q + QT, 0, :]).then_inc(out_stored, 16)

            def period(b):
                for e in range(E):
                    if e == 5 and b + 1 < B:
                        load_slots(b + 1, range(SLOT_RING))
                    store_expert(b, e)
                    if e == 1 and b + 3 < B:
                        load_x(b + 3)
                    if e == 5 and b > 0:
                        store_out(b - 1)
                    if e == 5 and b + 1 < B:
                        load_slots(b + 1, range(SLOT_RING, GROUPS))

            load_x(0)
            for i, w in ((2, Wr), (3, Wo)):
                sp.dma_start(w_raw[:, L * i:L * i + L, :], w.rearrange("l e d -> e l d")).then_inc(mix_weights_in, 16)
            load_expert(0)
            load_expert(1)
            load_x(1)
            sp.dma_start(router_sb[:, :], router_w).then_inc(router_in, 16)
            sp.dma_start(rbias_sb[:, :], router_b.partition_broadcast(P)).then_inc(router_in, 16)
            sp.wait_ge(zeroed, 1)
            for g in range(GROUPS):
                sp.dma_start(slot_view[g], slot_x[:, 0, :, :]).then_inc(rows_zeroed, 16)
            load_expert(2)
            load_expert(3)
            with nc.allow_non_contiguous_dma("per-feature columns"):
                sp.dma_start(bfc_sb[:, :, :], b_fc.rearrange("e a (c p) -> p e (a c)", p=P)).then_inc(small_in, 16)
                sp.dma_start(bgate_sb[:, :, :], b_gate.rearrange("e a (c p) -> p e (a c)", p=P)).then_inc(small_in, 16)
            for e in range(4, E):
                load_expert(e)
            sp.dma_start(bproj_sb[:, :, :], b_proj.rearrange("e a d -> (e a d)").partition_broadcast(P))\
              .then_inc(bproj_in, 16)
            for e in range(E):
                sp.dma_start(proj_sb[:, e, :, :], w_proj[e].rearrange("(c p) d -> p c d", p=P)).then_inc(proj_in, 16)
            load_x(2)
            load_slots(0, range(GROUPS))
            for b in range(B):
                period(b)
            store_out(B - 1)
            sp.wait_ge(out_stored, nth(B, 16 * QUARTERS, 0))

        @block.tensor
        def _(pe):
            def fill(stage, b, n, ps):
                for _ in range(FILL.get((stage, b, n), 0)):
                    nc.tensor.matmul(ps[:, :].rearrange("p (j d) -> p j d", d=P), ones[:, :],
                                     ones[:, :].rearrange("p (o d) -> p o d", o=1).to_broadcast([P, 4, P]),
                                     start=True, stop=True)

            def turn(b, n):
                last = n // 4
                between = banks_between(b)
                if not last and step(b, n) > between:
                    pe.wait_ge(r_copied, step(b, n) - between)
                if n == 0 and b >= 2:
                    pe.wait_ge(turned_sb[1], step(b - 1, 5))
                    pe.wait_ge(slots_copied, nth(b - 2, GROUPS, 4))
                if n == 4 and not later(b):
                    pe.wait_ge(x_added, step(b, 3))
                if n == 4 and later(b):
                    pe.wait_ge(r_copied, mixed_by(b))
                    pe.wait_ge(slots_copied, nth(b - 1, GROUPS, 1))
                if n == 5:
                    pe.wait_ge(turned_sb[1], step(b, 4))
                source = x_ln[:, b % RING, :, :] if last else normed
                ps = (route_banks(b) if last else mix_banks(b, n))[0]
                if b == 0 and n == 1:
                    pe.wait_ge(weights_copied, 2)
                fill("turn", b, n, ps)
                pe.wait_ge(normed_made[last], step(b, n))
                for j in range(HT):
                    mm = nc.tensor.transpose(ps[:, P * j:P * j + P], source[:, HT * (n % 2) + j, :], ident[:, :])
                mm.then_inc(turned_ps[last], 1)

            def kvr(b, n):
                half = slice(HALF * (n % 2), HALF * (n % 2) + HALF)
                layer = n // 2
                c = step(b, n)
                between = banks_between(b)
                ps_r, ps_k, ps_v = mix_banks(b, n)
                if c > between:
                    pe.wait_ge(k_copied, c - between)
                fill("kvr", b, n, ps_k)
                if c == 1:
                    pe.wait_ge(weights_copied, 2)
                pe.wait_ge(turned_sb[0], c)
                if n == 0 and b >= 2:
                    pe.wait_ge(rows_made, b)
                if n == 2 and b >= 2:
                    pe.wait_ge(x_added, step(b, 0))
                    pe.wait_ge(slots_copied, nth(b - 2, GROUPS, 5))
                nc.tensor.matmul(ps_k[:, :], w_mix[:, layer, :], normT[:, half], start=True, stop=True)\
                  .then_inc(k_made, 1)
                if c > between:
                    pe.wait_ge(kv_made, c - between)
                if n == 2 and b >= 2:
                    pe.wait_ge(x_added, step(b, 1))
                if n == 0 and b >= 2:
                    pe.wait_ge(logits_copied, nth(b - 1, 2, 2))
                nc.tensor.matmul(ps_v[:, :], w_mix[:, L + layer, :], normT[:, half], start=True, stop=True)\
                  .then_inc(v_made, 1)
                nc.tensor.matmul(ps_r[:, :], w_mix[:, 2 * L + layer, :], normT[:, half], start=True, stop=True)\
                  .then_inc(r_made, 1)

            def out(b, n):
                c = step(b, n)
                pe.wait_ge(mixed_made, c)
                if b == 0 and c > 2:
                    pe.wait_ge(x_added, c - 2)
                elif b == 1:
                    pe.wait_ge(x_added, c - 1)
                elif b > 1 and n % 2 == 0:
                    pe.wait_ge(k_copied, c + 1)
                elif b > 1:
                    pe.wait_ge(kv_made, c)
                for j in range(HT):
                    mm = nc.tensor.matmul(out_bank(b, n)[:, P * j:P * j + P],
                                          mixed[:, HALF * (n % 2) + P * j:HALF * (n % 2) + P * j + P],
                                          w_mix[:, 3 * L + n // 2, :], start=True, stop=True)
                mm.then_inc(out_made, 1)

            def logits(b, half):
                pe.wait_ge(router_in, 16 * 2)
                pe.wait_ge(turned_sb[1], step(b, 4 + half))
                if not later(b):
                    pe.wait_ge(turned_sb[1], step(b, 5))
                elif half == 0:
                    pe.wait_ge(x_added, mixed_by(b))
                    pe.wait_ge(slots_copied, nth(b - 1, GROUPS, 3))
                else:
                    pe.wait_ge(logits_copied, nth(b, 2, 1))
                for j in range(HT):
                    t = HT * half + j
                    mm = nc.tensor.matmul(route_banks(b)[2][:, E * t:E * t + E], route_turned(b)[:, P * t:P * t + P],
                                          router_sb[:, :], start=True, stop=True)
                mm.then_inc(logits_made, 1)

            def count(b, _):
                if later(b):
                    pe.wait_ge(x_added, mixed_by(b) - 1)
                    pe.wait_ge(slots_copied, nth(b - 1, GROUPS, 2))
                else:
                    pe.wait_ge(logits_copied, nth(b, 2, 2))
                pe.wait_ge(chosen_made, nth(b, 1, 1))
                counts = route_banks(b)[1][:, 0:TILES * K * E].rearrange("p (j k e) -> p j k e", k=K, e=E)
                nc.tensor.matmul(route_banks(b)[1][:, 0:TILES * K * E], upto[:, :],
                                 chosen[:, :, :, :].rearrange("p j k e -> p (j k e)"),
                                 start=True, stop=False, skip_group_check=True)
                for j in range(TILES - 1):
                    rest = TILES - 1 - j
                    for k in range(K):
                        nc.tensor.matmul(counts[:, j + 1:TILES, k, :], ones[:, :],
                                         chosen[:, j:j + 1, k, :].to_broadcast([P, rest, E]),
                                         start=False, stop=False, skip_group_check=True)
                for j in range(TILES):
                    mm = nc.tensor.matmul(counts[:, :, 1, :], ones[:, :],
                                          chosen[:, j:j + 1, 0, :].to_broadcast([P, TILES, E]),
                                          start=False, stop=(j == TILES - 1), skip_group_check=True)
                mm.then_inc(counts_made, 1)

            stages = {"turn": turn, "kvr": kvr, "out": out, "logits": logits, "count": count}

            def turn_slots(b, g):
                mixed = min(step(b + 1, 3), 4 * B)
                if g == 0:
                    pe.wait_ge(r_copied, mixed)
                    pe.wait_ge(turned_sb[1], step(b, 5))
                if g == 1:
                    pe.wait_ge(k_copied, mixed)
                    pe.wait_ge(x_added, mixed - 1)
                    pe.wait_ge(rows_made, b + 1)
                if g == 2:
                    pe.wait_ge(kv_made, mixed)
                    pe.wait_ge(x_added, mixed)
                    pe.wait_ge(logits_copied, nth(b, 2, 2))
                if g < 2 and later(b):
                    pe.wait_ge(slots_copied, nth(b - 1, GROUPS, 4 + g))
                if g >= 3:
                    pe.wait_ge(slots_copied, nth(b, GROUPS, g - 2))
                if g == 3 and b + 1 < B:
                    pe.wait_ge(turned_sb[1], step(b + 1, 5))
                if g == 4 and b + 1 < B:
                    pe.wait_ge(rows_made, b + 2)
                if g == 4 and b + 2 < B:
                    pe.wait_ge(x_added, step(b + 2, 0))
                fill("slots", b, g, bank[g % 3])
                pe.wait_ge(slots_loaded[g], nth(b, 16, 16))
                for j in range(4):
                    mm = nc.tensor.transpose(bank[g % 3][:, P * j:P * j + P], slot_x[:, g % SLOT_RING, j, :],
                                             ident[:, :])
                mm.then_inc(slots_turned, 1)

            def hidden_pair(b, e, j):
                c = e * HC + j
                cols = slice(e * SLOTS, e * SLOTS + COLS)
                chunk = slice(P * j, P * j + P)
                if j == 0:
                    pe.wait_ge(slots_copied, nth(b, GROUPS, (e * SLOTS + COLS - 1) // (4 * P) + 1))
                    if not later(b):
                        pe.wait_ge(weights_split, e + 1)
                if c == 0 and not later(b):
                    for read in (r_copied, k_copied, kv_made):
                        pe.wait_ge(read, nth(1, 4, 4))
                    pe.wait_ge(rows_made, 1)
                if c >= 2 or later(b):
                    pe.wait_ge(prod_made, nth(b, POINTS, c - 1))
                for which, (hi, lo, made) in enumerate(((gate_hi, gate_lo, g_made), (fc_hi, fc_lo, h_made))):
                    ps = pair[c % 2][which][:, 0:COLS]
                    nc.tensor.matmul(ps, hi[:, e, chunk], slotT_hi[:, cols], start=True, stop=False)
                    nc.tensor.matmul(ps, hi[:, e, chunk], slotT_lo[:, cols], start=False, stop=False)
                    nc.tensor.matmul(ps, lo[:, e, chunk], slotT_hi[:, cols], start=False, stop=True).then_inc(made, 1)

            def project(b, e, part):
                if part == 0:
                    pe.wait_ge(hidden_made, nth(b, 2 * E, 2 * e + 2))
                    if e or later(b):
                        pe.wait_ge(o_copied, nth(b, E, e))
                if not later(b) and e == 0 and part == 0:
                    pe.wait_ge(proj_in, 16 * E)
                    pe.wait_ge(x_added, step(1, 3))
                for c in range(HC):
                    mm = nc.tensor.matmul(ps_o[0:PART, P * part:P * part + P],
                                          hidden[:, e % 2, c, PART * part:PART * part + PART], proj_sb[:, e, c, :],
                                          start=(c == 0), stop=(c == HC - 1))
                if part == PARTS - 1:
                    mm.then_inc(o_made, 1)

            def period(b):
                for point in range(POINTS):
                    e, j = divmod(point, HC)
                    hidden_pair(b, e, j)
                    if b + 1 < B:
                        for name, n in TENSOR_ROUTE.get(point, ()):
                            stages[name](b + 1, n)
                    if e > 0:
                        for part in PROJECTIONS[b + 2 < B].get(j, ()):
                            project(b, e - 1, part)
                    if point == 1 and b > 0:
                        for part in range(PARTS):
                            project(b - 1, E - 1, part)
                    if point in SLOT_TURNS:
                        ahead, g = SLOT_TURNS[point]
                        if b + ahead < B:
                            turn_slots(b + ahead, g)
                    if b + 2 < B:
                        for name, n in TENSOR_MIX.get(point, ()):
                            stages[name](b + 2, n)

            pe.wait_ge(consts_made, 6)
            fill("weights", 0, 0, ps_o)
            pe.wait_ge(mix_weights_in, 16 * 4)
            for i in range(4 * L):
                mm = nc.tensor.transpose(pair[0][i // 4][:, P * (i % 4):P * (i % 4) + P], w_raw[:, i, :], ident[:, :])
            mm.then_inc(weights_turned, 1)
            for name, b, n in TENSOR_HEAD:
                stages[name](b, n)
            for g in range(3):
                turn_slots(0, g)
            for b in range(B):
                period(b)
            for part in range(PARTS):
                project(B - 1, E - 1, part)

        @block.scalar
        def _(act):
            def turned(b, n):
                half = n % 2
                last = n // 4
                act.wait_ge(turned_ps[last], step(b, n))
                if last and later(b):
                    act.wait_ge(r_made, mixed_by(b) - 1 + half)
                elif not last and step(b, n) > 2:
                    act.wait_ge(r_made, step(b, n) - 2)
                if n < 2 and b >= 2:
                    act.wait_ge(logits_made, nth(b - 1, 2, half + 1))
                if last and not later(b):
                    act.wait_ge(weights_turned, 1)
                tokens = slice(HALF * half, HALF * half + HALF)
                if not last:
                    nc.scalar.activation(normT[:, tokens], mix_banks(b, n)[0][:, :], ACT.Identity,
                                         bias=lnb_sb[:, n // 2:n // 2 + 1],
                                         scale=lnw_sb[:, n // 2:n // 2 + 1]).then_inc(turned_sb[0], 1)
                else:
                    nc.scalar.activation(route_turned(b)[:, tokens], route_banks(b)[0][:, :], ACT.Copy)\
                      .then_inc(turned_sb[1], 1)

            def kr(b, n):
                half = slice(HALF * (n % 2), HALF * (n % 2) + HALF)
                c = step(b, n)
                act.wait_ge(k_made, c)
                if c > 2:
                    act.wait_ge(state_made, c - 2)
                nc.scalar.activation(kv_sb[:, half], mix_banks(b, n)[1][:, :], ACT.Copy, scale=(1.0 - DECAY) / 2)\
                  .then_inc(k_copied, 1)
                act.wait_ge(r_made, c)
                if c > 2:
                    act.wait_ge(out_made, c - 2)
                nc.scalar.activation(mixed[:, half], mix_banks(b, n)[0][:, :], ACT.Tanh, scale=0.5)\
                  .then_inc(r_copied, 1)

            def lead(b, _):
                act.wait_ge(gap_made, nth(b, 1, 1))
                if later(b):
                    act.wait_ge(share_made, nth(b - 1, 1, 1))
                nc.scalar.activation(gap_t[:, :], gap[:, :], ACT.Tanh, scale=0.5).then_inc(gap_turned, 1)

            stages = {"turned": turned, "kr": kr, "lead": lead}

            def copy_slots(b, g):
                act.wait_ge(slots_turned, nth(b, GROUPS, g + 1))
                if later(b):
                    act.wait_ge(h_made, nth(b - 1, POINTS, HC * min(E, (4 * P * (g + 1) - 1) // SLOTS + 1)))
                nc.scalar.activation(slotT_hi[:, 4 * P * g:4 * P * g + 4 * P], bank[g % 3][:, :], ACT.Copy)\
                  .then_inc(slots_high, 1)

            def high(e, _):
                act.wait_ge(expert_weights_in[e % 2], 32 * (e // 2 + 1))
                nc.scalar.activation(gate_hi[:, e, :], w_in[:, e % 2, 0:H], ACT.Copy)
                nc.scalar.activation(fc_hi[:, e, :], w_in[:, e % 2, H:2 * H], ACT.Copy).then_inc(weights_high, 1)

            def gate_copy(b, e, j):
                c = e * HC + j
                act.wait_ge(g_made, nth(b, POINTS, c + 1))
                if c == 0 and not later(b):
                    act.wait_ge(small_in, 16 * 2)
                if c >= 2 or later(b):
                    act.wait_ge(prod_made, nth(b, POINTS, c - 1))
                nc.scalar.activation(gate_s[:, c % 2, :], pair[c % 2][0][:, 0:COLS], ACT.Identity,
                                     bias=bgate_sb[:, e, j:j + 1]).then_inc(g_copied, 1)

            def silu(b, e, i):
                act.wait_ge(prod_made, nth(b, POINTS, e * HC + 2 * i + 2))
                if e >= 2 or later(b):
                    act.wait_ge(o_made, nth(b, E, e - 1))
                nc.scalar.activation(hidden[:, e % 2, 2 * i:2 * i + 2, 0:COLS], prod[:, e % 2, 2 * i:2 * i + 2, :],
                                     ACT.Silu).then_inc(hidden_made, 1)

            stages["high"] = high

            def period(b):
                for point in range(POINTS):
                    e, j = divmod(point, HC)
                    gate_copy(b, e, j)
                    if j == 0 and e > 0:
                        silu(b, e - 1, 1)
                    if point == 0 and b > 0:
                        silu(b - 1, E - 1, 1)
                    if j == 2:
                        silu(b, e, 0)
                    if b + 1 < B:
                        for name, n in SCALAR_ROUTE.get(point, ()):
                            stages[name](b + 1, n)
                    if point in SLOT_TURNS:
                        ahead, g = SLOT_TURNS[point]
                        if b + ahead < B:
                            copy_slots(b + ahead, g)
                    if b + 2 < B:
                        for name, n in SCALAR_MIX.get(point, ()):
                            stages[name](b + 2, n)

            for i, w in enumerate((Wk, Wv)):
                act.dma_start(w_raw[:, L * i:L * i + L, :], w.rearrange("l e d -> e l d")).then_inc(mix_weights_in, 16)
            with nc.allow_non_contiguous_dma("per-feature columns"):
                act.dma_start(lnw_sb[:, :], ln_w.rearrange("l d -> d l")).then_inc(ln_in, 16)
                act.dma_start(lnb_sb[:, :], ln_b.rearrange("l d -> d l")).then_inc(ln_in, 16)
            act.wait_ge(vector_consts, 2)
            nc.scalar.activation(gap_t[:, :], decay[:, 0:TILES], ACT.Silu)
            act.wait_ge(weights_turned, 1)
            for i in range(2):
                nc.scalar.activation(w_mix[:, 4 * i:4 * i + 4, :],
                                     pair[0][i][:, :].rearrange("p (w d) -> p w d", w=4), ACT.Copy)\
                  .then_inc(weights_copied, 1)
            act.wait_ge(ln_in, 32)
            for name, b, n in SCALAR_HEAD:
                stages[name](b, n)
            for g in range(3):
                copy_slots(0, g)
            for b in range(B):
                period(b)
            silu(B - 1, E - 1, 1)

        @block.vector
        def _(dve):
            def source_of(b, n):
                return (x_in, x_mid, x_in)[n // 2][:, b % 2, :, :]

            def stats_of(b, n):
                norm, half = divmod(n, 2)
                r, last = b % 2, n // 4
                if n == 0:
                    dve.wait_ge(x_loaded[r], 16 * (b // 2 + 1))
                if norm > 0:
                    dve.wait_ge(x_added, step(b, n - 2))
                if b >= 2:
                    dve.wait_ge(normed_made[last], step(b - 2, n))
                for j in range(HT * half, HT * half + HT):
                    i = nc.vector.bn_stats(stats[:, r, norm, j, :], source_of(b, n)[:, j, :])
                i.then_inc(stats_made[last], 1)
                dve.wait_ge(stats_made[last], step(b, n))
                for j in range(HT * half, HT * half + HT):
                    i = nc.vector.bn_aggr(moments[:, r, norm, j, :], stats[:, r, norm, j, :])
                i.then_inc(moments_made[last], 1)

            def norm_of(b, n):
                norm, half = divmod(n, 2)
                r, last = b % 2, n // 4
                dve.wait_ge(rstd_made[last], step(b, n))
                if not last and step(b, n) > 2:
                    dve.wait_ge(turned_ps[0], step(b, n) - 2)
                if last and b >= RING:
                    dve.wait_ge(y_made, nth(b - RING, QUARTERS, QUARTERS))
                dve.wait_ge(moments_made[last], step(b, n))
                dst = x_ln[:, b % RING, :, :] if last else normed
                for j in range(HT * half, HT * half + HT):
                    i = nc.vector.tensor_scalar(dst[:, j, :], source_of(b, n)[:, j, :], moments[:, r, norm, j, 0:1],
                                                rstd[:, r, norm, j:j + 1], ALU.subtract, ALU.mult)
                i.then_inc(normed_made[last], 1)

            def skip_sum(b, _):
                dve.wait_ge(x_added, step(b, 1))
                dve.wait_ge(normed_made[0], step(b, 1))
                nc.vector.tensor_tensor(x_in[:, b % 2, :, :], x_in[:, b % 2, :, :], x_mid[:, b % 2, :, :], ALU.add)\
                  .then_inc(skip_made, 1)

            def mix(b, n):
                lo, hi = HALF * (n % 2), HALF * (n % 2) + HALF
                c = step(b, n)
                dve.wait_ge(k_copied, c)
                dve.wait_ge(v_made, c)
                nc.vector.tensor_tensor(kv_sb[:, lo:hi], mix_banks(b, n)[2][:, :], kv_sb[:, lo:hi], ALU.mult)\
                  .then_inc(kv_made, 1)
                dve.wait_ge(kv_made, c)
                if c > 1:
                    dve.wait_ge(mixed_made, c - 1)
                nc.vector.tensor_tensor_scan(state[:, lo:hi], decay[:, :], kv_sb[:, lo:hi],
                                             state[:, lo - 1:lo] if n % 2 else 0.0, ALU.mult, ALU.add)\
                  .then_inc(state_made, 1)
                dve.wait_ge(r_copied, c)
                dve.wait_ge(state_made, c)
                nc.vector.scalar_tensor_tensor(mixed[:, lo:hi], mixed[:, lo:hi], 1.0, state[:, lo:hi],
                                               ALU.add, ALU.mult).then_inc(mixed_made, 1)

            def add(b, n):
                layer, half = divmod(n, 2)
                tiles = slice(HT * half, HT * half + HT)
                src = x_in[:, b % 2, tiles, :]
                dve.wait_ge(out_made, step(b, n))
                if layer == 0:
                    if b >= 2:
                        dve.wait_ge(skip_made, b - 1)
                        dve.wait_ge(normed_made[0], step(b - 2, 2 + half))
                    dst = x_mid[:, b % 2, tiles, :]
                else:
                    dve.wait_ge(skip_made, b + 1)
                    dst = src
                nc.vector.tensor_tensor(dst, src, out_bank(b, n)[:, :].rearrange("p (j d) -> p j d", d=P), ALU.add)\
                  .then_inc(x_added, 1)

            def slots_low(b, g):
                cols = slice(4 * P * g, 4 * P * g + 4 * P)
                dve.wait_ge(slots_high, nth(b, GROUPS, g + 1))
                nc.vector.tensor_tensor(slotT_lo[:, cols], bank[g % 3][:, :], slotT_hi[:, cols].bitcast(F32),
                                        ALU.subtract).then_inc(slots_copied, 1)

            def top(b, half):
                tiles = range(HT * half, HT * half + HT)
                dve.wait_ge(router_in, 16 * 2)
                dve.wait_ge(logits_made, nth(b, 2, half + 1 if later(b) else 2))
                if later(b):
                    dve.wait_ge(top_index_made, nth(b - 1, 2, half + 1))
                nc.vector.tensor_tensor(logit[:, HT * half:HT * half + HT, :],
                                        route_banks(b)[2][:, HT * E * half:HT * E * half + HT * E]
                                        .rearrange("p (j e) -> p j e", e=E),
                                        rbias_sb[:, :].rearrange("p (o e) -> p o e", o=1).to_broadcast([P, HT, E]),
                                        ALU.add).then_inc(logits_copied, 1)
                dve.wait_ge(logits_copied, nth(b, 2, half + 1))
                if later(b):
                    dve.wait_ge(gap_made, nth(b - 1, 1, 1))
                for j in tiles:
                    i = nc.vector.max(top_v[:, j, :], logit[:, j, :])
                i.then_inc(top_made, 1)
                dve.wait_ge(top_made, nth(b, 2, half + 1))
                if later(b):
                    dve.wait_ge(top_copied, nth(b - 1, 1, 1))
                for j in tiles:
                    i = nc.vector.max_index(top_i[:, j, :], top_v[:, j, :], logit[:, j, :])
                i.then_inc(top_index_made, 1)

            def choice(b, _):
                dve.wait_ge(top_made, nth(b, 2, 2))
                if later(b):
                    dve.wait_ge(gap_turned, nth(b - 1, 1, 1))
                nc.vector.tensor_tensor(gap[:, :], top_v[:, :, 0:1].rearrange("p j o -> p (j o)"),
                                        top_v[:, :, 1:2].rearrange("p j o -> p (j o)"), ALU.subtract)\
                  .then_inc(gap_made, 1)
                dve.wait_ge(top_index_made, nth(b, 2, 2))
                if later(b):
                    dve.wait_ge(chosen_made, nth(b - 1, 1, 1))
                nc.vector.tensor_copy(top_f[:, :, :], top_i[:, :, 0:K]).then_inc(top_copied, 1)
                dve.wait_ge(top_copied, nth(b, 1, 1))
                dve.wait_ge(consts_made, 6)
                if later(b):
                    dve.wait_ge(rows_made, nth(b - 1, 1, 1))
                nc.vector.tensor_tensor(
                    chosen[:, :, :, :].rearrange("p j k e -> p (j k) e"),
                    expert_id[:, :].rearrange("p (c e) -> p c e", e=E),
                    top_f[:, :, :].rearrange("p j (k o) -> p (j k) o", o=1).to_broadcast([P, TILES * K, E]),
                    ALU.is_equal).then_inc(chosen_made, 1)

            def rows(b, _):
                counts = route_banks(b)[1][:, 0:TILES * K * E]
                picks = chosen[:, :, :, :].rearrange("p j k e -> p (j k) e")
                dve.wait_ge(counts_made, nth(b, 1, 1))
                dve.wait_ge(chosen_made, nth(b, 1, 1))
                nc.vector.scalar_tensor_tensor(row_in[:, :], counts, float(CAP), expert_base[:, :],
                                               ALU.min, ALU.add).then_inc(rows_step, 1)
                nc.vector.tensor_scalar(row_far[:, :], counts, float(CAP), FAR, ALU.is_gt, ALU.mult)\
                  .then_inc(rows_step, 1)
                dve.wait_ge(rows_step, nth(b, 5, 2))
                nc.vector.tensor_tensor(row_both[:, 0, :, :], row_in[:, :].rearrange("p (c e) -> p c e", e=E),
                                        picks, ALU.mult).then_inc(rows_step, 1)
                nc.vector.tensor_tensor(row_far[:, :], row_far[:, :], row_in[:, :], ALU.add).then_inc(rows_step, 1)
                dve.wait_ge(rows_step, nth(b, 5, 4))
                nc.vector.tensor_tensor(row_both[:, 1, :, :], row_far[:, :].rearrange("p (c e) -> p c e", e=E),
                                        picks, ALU.mult).then_inc(rows_step, 1)
                dve.wait_ge(rows_step, nth(b, 5, 5))
                nc.vector.tensor_reduce(row_f[:, :, :].rearrange("p w c -> p (w c)"),
                                        row_both[:, :, :, :].rearrange("p w c e -> p (w c) e"), AX.X, ALU.add)\
                  .then_inc(rows_reduced, 1)
                dve.wait_ge(rows_reduced, nth(b, 1, 1))
                if b >= RING:
                    for q in range(QUARTERS):
                        dve.wait_ge(gathered[q], nth(b - RING, 16 * K * QT, 16 * K * QT))
                if later(b):
                    dve.wait_ge(scattered, nth(b - 1, 16 * TILES * K, 16 * TILES * K))
                nc.vector.tensor_copy(row_from[:, b % RING, :], row_f[:, 0, :])
                nc.vector.tensor_copy(row_to[:, :], row_f[:, 1, :]).then_inc(rows_made, 1)

            stages = {"stats": stats_of, "norm": norm_of, "mix": mix, "skip_sum": skip_sum, "add": add, "top": top,
                      "choice": choice, "rows": rows}

            def gather_sum(b, q):
                dve.wait_ge(gathered[q], nth(b, 16 * K * QT, 16 * K * QT))
                dve.wait_ge(share_made, nth(b, 1, 1))
                for j in range(QT * q, QT * q + QT):
                    i = nc.vector.scalar_tensor_tensor(picked[:, j, 0, :], picked[:, j, 0, :],
                                                       share[:, b % RING, j, 0:1],
                                                       x_ln[:, b % RING, j, :], ALU.mult, ALU.add)
                i.then_inc(part_made, 1)
                dve.wait_ge(part_made, nth(b, QUARTERS, q + 1))
                for j in range(QT * q, QT * q + QT):
                    i = nc.vector.scalar_tensor_tensor(picked[:, j, 1, :], picked[:, j, 1, :],
                                                       share[:, b % RING, j, 1:2],
                                                       picked[:, j, 0, :], ALU.mult, ALU.add)
                i.then_inc(y_made, 1)
                dve.wait_ge(y_made, nth(b, QUARTERS, q + 1))
                for j in range(QT * q, QT * q + QT):
                    i = nc.vector.bn_stats(y_stats[:, j, :], picked[:, j, 1, :])
                i.then_inc(y_stats_made, 1)
                dve.wait_ge(y_stats_made, nth(b, QUARTERS, q + 1))
                for j in range(QT * q, QT * q + QT):
                    i = nc.vector.bn_aggr(y_moments[:, j, :], y_stats[:, j, :])
                i.then_inc(y_moments_made, 1)

            def final_norm(b, q):
                dve.wait_ge(y_rstd_made, nth(b, QUARTERS, q + 1))
                dve.wait_ge(y_moments_made, nth(b, QUARTERS, q + 1))
                for j in range(QT * q, QT * q + QT):
                    i = nc.vector.tensor_scalar(picked[:, j, 0, :], picked[:, j, 1, :], y_moments[:, j, 0:1],
                                                y_rstd[:, j:j + 1], ALU.subtract, ALU.mult)
                i.then_inc(y_normed, 1)

            combine_stages = {"gather_sum": gather_sum, "final_norm": final_norm}

            def product(b, e, j):
                c = e * HC + j
                dve.wait_ge(h_made, nth(b, POINTS, c + 1))
                dve.wait_ge(g_copied, nth(b, POINTS, c + 1))
                if c == 0 and not later(b):
                    dve.wait_ge(weights_split, E)
                if j == 0 and (e >= 2 or later(b)):
                    dve.wait_ge(hidden_made, nth(b, 2 * E, 2 * e - 2))
                nc.vector.scalar_tensor_tensor(prod[:, e % 2, j, :], pair[c % 2][1][:, 0:COLS], bfc_sb[:, e, j:j + 1],
                                               gate_s[:, c % 2, :], ALU.add, ALU.mult).then_inc(prod_made, 1)

            def copy_out(b, e):
                dve.wait_ge(o_made, nth(b, E, e + 1))
                dve.wait_ge(bproj_in, 16)
                c = b * E + e
                if c >= OUT_RING:
                    dve.wait_ge(o_stored[c % OUT_RING], 16 * (c // OUT_RING))
                nc.vector.tensor_tensor(o_sb[:, c % OUT_RING, :, :],
                                        ps_o[0:PART, 0:PARTS * P].rearrange("p (i d) -> p i d", d=P),
                                        bproj_sb[0:PART, e:e + 1, :].to_broadcast([PART, PARTS, P]), ALU.add)\
                  .then_inc(o_copied, 1)

            def period(b):
                for point in range(POINTS):
                    e, j = divmod(point, HC)
                    if j == 0 and e > 1:
                        copy_out(b, e - 2)
                    if point in (0, 2) and b > 0:
                        copy_out(b - 1, E - 2 + point // 2)
                    product(b, e, j)
                    if point in SLOT_TURNS:
                        ahead, g = SLOT_TURNS[point]
                        if b + ahead < B:
                            slots_low(b + ahead, g)
                    if b > 0:
                        for name, n in (VECTOR_COMBINE if b + 2 < B else VECTOR_COMBINE_LATE).get(point, ()):
                            combine_stages[name](b - 1, n)
                    if b + 1 < B:
                        for name, n in VECTOR_ROUTE.get(point, ()):
                            stages[name](b + 1, n)
                    if b + 2 < B:
                        for name, n in VECTOR_MIX.get(point, ()):
                            stages[name](b + 2, n)
                    if b + 3 < B:
                        for name, n in VECTOR_AHEAD.get(point, ()):
                            stages[name](b + 3, n)

            nc.vector.memset(decay[:, :], DECAY).then_inc(vector_consts, 1)
            nc.vector.memset(hidden[:, :, :, :], 0.0).then_inc(vector_consts, 1)
            dve.wait_ge(vector_consts, 2)
            for name, b, n in VECTOR_HEAD:
                stages[name](b, n)
            for g in range(3):
                slots_low(0, g)
            for b in range(B):
                period(b)
            copy_out(B - 1, E - 2)
            copy_out(B - 1, E - 1)
            for name, q in VECTOR_TAIL:
                combine_stages[name](B - 1, q)

        @block.gpsimd
        def _(pool):
            def rstd_of(b, n):
                norm, half = divmod(n, 2)
                r, last = b % 2, n // 4
                tiles = slice(HT * half, HT * half + HT)
                pool.wait_ge(moments_made[last], step(b, n))
                nc.gpsimd.tensor_scalar(shifted[:, r, norm, tiles],
                                        moments[:, r, norm, tiles, 1:2].rearrange("p j o -> p (j o)"),
                                        EPS, None, ALU.add).then_inc(shifted_made[last], 1)
                pool.wait_ge(shifted_made[last], step(b, n))
                nc.gpsimd.tensor_tensor(rstd[:, r, norm, tiles], shifted[:, r, norm, tiles], power[:, :], ALU.pow)\
                  .then_inc(rstd_made[last], 1)

            def shares(b, _):
                pool.wait_ge(gap_turned, nth(b, 1, 1))
                if b >= RING:
                    pool.wait_ge(y_made, nth(b - RING, QUARTERS, QUARTERS))
                nc.gpsimd.tensor_scalar(share[:, b % RING, :, 0:1].rearrange("p j o -> p (j o)"), gap_t[:, :], 0.5, 0.5,
                                        ALU.mult, ALU.add)
                nc.gpsimd.tensor_scalar(share[:, b % RING, :, 1:2].rearrange("p j o -> p (j o)"), gap_t[:, :],
                                        -0.5, 0.5, ALU.mult, ALU.add).then_inc(share_made, 1)

            def scatter(b, j):
                if j == 0:
                    pool.wait_ge(rows_made, nth(b, 1, 1))
                    pool.wait_ge(normed_made[1], step(b, 5))
                    if later(b):
                        for g in range(GROUPS):
                            pool.wait_ge(slots_loaded[g], nth(b - 1, 16, 16))
                    else:
                        pool.wait_ge(rows_zeroed, 16 * GROUPS)
                for k in range(K):
                    c = j * K + k
                    nc.gpsimd.indirect_dma_start(
                        out=slot_rows, out_offset=bass.IndirectOffsetOnAxis(ap=row_to[:, c:c + 1], axis=0),
                        in_=x_ln[:, b % RING, j, :], in_offset=None, bounds_check=ROWS - 1, oob_is_err=False)\
                      .then_inc(scattered, 16)

            def low(e, _):
                pool.wait_ge(weights_high, e + 1)
                nc.gpsimd.tensor_tensor(gate_lo[:, e, :], w_in[:, e % 2, 0:H], gate_hi[:, e, :].bitcast(F32),
                                        ALU.subtract)
                nc.gpsimd.tensor_tensor(fc_lo[:, e, :], w_in[:, e % 2, H:2 * H], fc_hi[:, e, :].bitcast(F32),
                                        ALU.subtract).then_inc(weights_split, 1)

            stages = {"low": low, "rstd": rstd_of, "shares": shares, "scatter": scatter}

            def gather(b, j):
                q = j // QT
                if j == 0:
                    for i in range(OUT_RING):
                        pool.wait_ge(o_stored[i], 16 * stored(b, i))
                    if later(b):
                        pool.wait_ge(out_stored, nth(b, 16 * QUARTERS, 0))
                    else:
                        pool.wait_ge(weights_turned, 1)
                        pool.wait_ge(logits_made, 2)
                for k in range(K):
                    c = j * K + k
                    nc.gpsimd.indirect_dma_start(
                        out=picked[:, j, k, :], out_offset=None, in_=expert_rows,
                        in_offset=bass.IndirectOffsetOnAxis(ap=row_from[:, b % RING, c:c + 1], axis=0),
                        bounds_check=E * SLOTS - 1, oob_is_err=False).then_inc(gathered[q], 16)

            def final_rstd(b, q):
                tiles = slice(QT * q, QT * q + QT)
                pool.wait_ge(y_moments_made, nth(b, QUARTERS, q + 1))
                if later(b):
                    pool.wait_ge(y_normed, nth(b, QUARTERS, 0))
                nc.gpsimd.tensor_scalar(y_shifted[:, tiles],
                                        y_moments[:, tiles, 1:2].rearrange("p j o -> p (j o)"),
                                        EPS, None, ALU.add).then_inc(y_shifted_made, 1)
                pool.wait_ge(y_shifted_made, nth(b, QUARTERS, q + 1))
                nc.gpsimd.tensor_tensor(y_rstd[:, tiles], y_shifted[:, tiles], power[:, 0:QT], ALU.pow)\
                  .then_inc(y_rstd_made, 1)

            combine_stages = {"gather": gather, "final_rstd": final_rstd}

            def period(b):
                for point in range(POINTS):
                    if b > 0:
                        for name, n in POOL_COMBINE.get(point, ()):
                            combine_stages[name](b - 1, n)
                    if b + 1 < B:
                        for name, n in POOL_ROUTE.get(point, ()):
                            stages[name](b + 1, n)
                    if b + 2 < B:
                        for name, n in POOL_MIX.get(point, ()):
                            stages[name](b + 2, n)
                    if b + 3 < B:
                        for name, n in POOL_AHEAD.get(point, ()):
                            stages[name](b + 3, n)

            nc.gpsimd.memset(slot_x[:, 0, :, :], 0.0).then_inc(zeroed, 1)
            nc.gpsimd.memset(ident[:, :], 0.0).then_inc(pool_consts, 1)
            nc.gpsimd.memset(ones[:, :], 1.0).then_inc(consts_made, 1)
            nc.gpsimd.memset(power[:, :], -0.5).then_inc(consts_made, 1)
            nc.gpsimd.memset(upto[:, :], 1.0).then_inc(pool_consts, 1)
            pool.wait_ge(pool_consts, 2)
            nc.gpsimd.affine_select(out=ident[:, :], in_=ident[:, :], compare_op=ALU.not_equal, fill=1.0, base=0,
                                    pattern=[[-1, P]], channel_multiplier=1).then_inc(consts_made, 1)
            nc.gpsimd.affine_select(out=upto[:, :], in_=upto[:, :], compare_op=ALU.is_ge, fill=0.0, base=0,
                                    pattern=[[1, P]], channel_multiplier=-1).then_inc(consts_made, 1)
            nc.gpsimd.iota(expert_id[:, :], pattern=[[0, TILES * K], [1, E]], base=0, channel_multiplier=0,
                           allow_small_or_imprecise_dtypes=True).then_inc(consts_made, 1)
            nc.gpsimd.iota(expert_base[:, :], pattern=[[0, TILES * K], [SLOTS, E]], base=-1, channel_multiplier=0,
                           allow_small_or_imprecise_dtypes=True).then_inc(consts_made, 1)
            pool.wait_ge(consts_made, 6)
            for name, b, n in POOL_HEAD:
                stages[name](b, n)
            for b in range(B):
                period(b)
            for name, n in POOL_TAIL:
                combine_stages[name](B - 1, n)


_INPUTS = ["L0_attn_h", "L0_attn_ln_w", "L0_attn_ln_b", "L0_attn_Wk", "L0_attn_Wv", "L0_attn_Wr", "L0_attn_Wo",
           "L0_ffn_router_w", "L0_ffn_router_b", "L0_ffn_w_c_fc", "L0_ffn_b_c_fc", "L0_ffn_w_gate",
           "L0_ffn_b_gate", "L0_ffn_w_c_proj", "L0_ffn_b_c_proj"]


def kernel(**inputs):
    import concourse.bacc as bacc
    from concourse.bass_utils import run_bass_kernel_spmd

    nc = bacc.Bacc("TRN2", target_bir_lowering=False, num_devices=1)
    arrays, args = {}, []
    for name in _INPUTS:
        a = np.ascontiguousarray(inputs[name])
        arrays[f"in_{name}"] = a
        args.append(nc.dram_tensor(f"in_{name}", a.shape, mybir.dt.from_np(a.dtype), kind="ExternalInput").ap())
    args.append(nc.dram_tensor("out_0", (B, T, P), F32, kind="ExternalOutput").ap())
    time_mix_moe(nc, *args)
    r = run_bass_kernel_spmd(nc, [arrays], core_ids=[0])
    return r.results[0]["out_0"]
```
